# Optimizing a Trainium2 kernel written in Bass

```python
import numpy as np
import jax
import jax.numpy as jnp

def _softmax(x, axis=-1):
    return jax.nn.softmax(x, axis=axis)

def _gelu(x):
    return jax.nn.gelu(x, approximate=True)

def _silu(x):
    return jax.nn.silu(x)

def _sigmoid(x):
    return jax.nn.sigmoid(x)

def _layernorm(x, axis=-1, eps=1e-05):
    m = jnp.mean(x, axis=axis, keepdims=True)
    v = jnp.var(x, axis=axis, keepdims=True)
    return (x - m) / jnp.sqrt(v + eps)

def _scatter_add(tgt, idx, src, axis=0):
    return tgt.at[idx].add(src)

def _segment_sum(src, seg, n):
    return jax.ops.segment_sum(src, seg, n)
kernel_name = 'mk_gnn_preln_d2_gnn_r64_f84491'

def setup_inputs(seed: int=0):
    np.random.seed(seed)
    _w = jnp.asarray

    def _rec_inputs():
        import jax
        import jax.numpy as jnp
        _gk = jax.random.key(seed)
        x = -0.0001006 + 1 * jax.random.normal(jax.random.fold_in(_gk, 1), (100000, 96), jnp.float32)
        src = jax.random.randint(jax.random.fold_in(_gk, 2), (50000,), 0, 100000, jnp.int32)
        dst = jnp.minimum((100000 * jax.random.uniform(jax.random.fold_in(_gk, 3), (50000,)) ** 2.0).astype(jnp.int32), 99999)
        _o = jnp.argsort(dst, stable=True)
        src = src[_o]
        dst = dst[_o]
        edge_attr_96 = 5.93493e-05 + 1.00006 * jax.random.normal(jax.random.fold_in(_gk, 11), (50000, 96), jnp.float32)
        return (x, src, dst, edge_attr_96)
    x, src, dst, edge_attr_96 = _rec_inputs()

    def _L0_gnn_setup():
        import jax, jax.numpy as jnp
        import numpy as np
        N_NODES = 50000
        N_EDGES = 12500
        D = 96
        LN_EPS = 1e-05

        def _layer(h, src, dst, norm, n_nodes, W, b, g, be):
            h = h @ W
            msg = h[src] * norm[:, None]
            h = jax.ops.segment_sum(msg, dst, num_segments=n_nodes) + b
            h = jnp.tanh(h)
            mu = jnp.mean(h, axis=-1, keepdims=True)
            var = jnp.mean(jnp.square(h - mu), axis=-1, keepdims=True)
            h = (h - mu) * jax.lax.rsqrt(var + LN_EPS)
            return h * g + be
        key = jax.random.key(seed)
        ks = jax.random.split(key, 4)
        x = jax.random.normal(ks[0], (N_NODES, D), dtype=jnp.float32)
        edge_index = jax.random.randint(ks[1], (2, N_EDGES), 0, N_NODES, dtype=jnp.int64)
        scale = 1.0 / np.sqrt(D)
        W0 = jax.random.normal(ks[2], (D, D), dtype=jnp.float32) * scale
        W1 = jax.random.normal(ks[3], (D, D), dtype=jnp.float32) * scale
        b0 = jnp.zeros((D,), jnp.float32)
        b1 = jnp.zeros((D,), jnp.float32)
        g0 = jnp.ones((D,), jnp.float32)
        g1 = jnp.ones((D,), jnp.float32)
        be0 = jnp.zeros((D,), jnp.float32)
        be1 = jnp.zeros((D,), jnp.float32)
        return {'x': x, 'edge_index': edge_index, 'W0': W0, 'b0': b0, 'g0': g0, 'be0': be0, 'W1': W1, 'b1': b1, 'g1': g1, 'be1': be1}
    _L0_gnn_all = _L0_gnn_setup()
    _L0_gnn_in = {k: v for k, v in _L0_gnn_all.items() if k in ('W0', 'b0', 'g0', 'be0', 'W1', 'b1', 'g1', 'be1')}
    del _L0_gnn_all

    def _L1_gnn_setup():
        import jax, jax.numpy as jnp
        import numpy as np
        N_NODES = 50000
        N_EDGES = 12500
        DIM = 96
        key = jax.random.key(seed)
        k = jax.random.split(key, 6)
        x = jax.random.normal(k[0], (N_NODES, DIM), dtype=jnp.float32)
        edge_index = jax.random.randint(k[1], (2, N_EDGES), 0, N_NODES, dtype=jnp.int64)
        edge_attr = jax.random.normal(k[2], (N_EDGES, DIM), dtype=jnp.float32)
        scale = 1.0 / np.sqrt(DIM)
        W1 = jax.random.normal(k[3], (DIM, DIM), dtype=jnp.float32) * scale
        b1 = jnp.zeros((DIM,), dtype=jnp.float32)
        W2 = jax.random.normal(k[4], (DIM, DIM), dtype=jnp.float32) * scale
        b2 = jnp.zeros((DIM,), dtype=jnp.float32)
        return {'x': x, 'edge_index': edge_index, 'edge_attr': edge_attr, 'W1': W1, 'b1': b1, 'W2': W2, 'b2': b2}
    _L1_gnn_all = _L1_gnn_setup()
    _L1_gnn_in = {k: v for k, v in _L1_gnn_all.items() if k in ('W1', 'b1', 'W2', 'b2')}
    del _L1_gnn_all
    return {'x': x, 'src': src, 'dst': dst, 'edge_attr_96': edge_attr_96, 'L0_gnn_W0': _L0_gnn_in['W0'], 'L0_gnn_b0': _L0_gnn_in['b0'], 'L0_gnn_g0': _L0_gnn_in['g0'], 'L0_gnn_be0': _L0_gnn_in['be0'], 'L0_gnn_W1': _L0_gnn_in['W1'], 'L0_gnn_b1': _L0_gnn_in['b1'], 'L0_gnn_g1': _L0_gnn_in['g1'], 'L0_gnn_be1': _L0_gnn_in['be1'], 'L1_gnn_W1': _L1_gnn_in['W1'], 'L1_gnn_b1': _L1_gnn_in['b1'], 'L1_gnn_W2': _L1_gnn_in['W2'], 'L1_gnn_b2': _L1_gnn_in['b2']}

def reference(x, src, dst, edge_attr_96, L0_gnn_W0, L0_gnn_b0, L0_gnn_g0, L0_gnn_be0, L0_gnn_W1, L0_gnn_b1, L0_gnn_g1, L0_gnn_be1, L1_gnn_W1, L1_gnn_b1, L1_gnn_W2, L1_gnn_b2):
    import jax
    import jax.numpy as jnp

    def _L0_gnn_ref(x, edge_index, W0, b0, g0, be0, W1, b1, g1, be1):
        import jax, jax.numpy as jnp
        import numpy as np
        N_NODES = 50000
        N_EDGES = 12500
        D = 96
        LN_EPS = 1e-05

        def _layer(h, src, dst, norm, n_nodes, W, b, g, be):
            h = h @ W
            msg = h[src] * norm[:, None]
            h = jax.ops.segment_sum(msg, dst, num_segments=n_nodes) + b
            h = jnp.tanh(h)
            mu = jnp.mean(h, axis=-1, keepdims=True)
            var = jnp.mean(jnp.square(h - mu), axis=-1, keepdims=True)
            h = (h - mu) * jax.lax.rsqrt(var + LN_EPS)
            return h * g + be
        n = x.shape[0]
        loops = jnp.arange(n, dtype=edge_index.dtype)
        src = jnp.concatenate([edge_index[0], loops])
        dst = jnp.concatenate([edge_index[1], loops])
        deg = jax.ops.segment_sum(jnp.ones(src.shape, x.dtype), dst, num_segments=n)
        dis = jax.lax.rsqrt(deg)
        norm = dis[src] * dis[dst]
        h = _layer(x, src, dst, norm, n, W0, b0, g0, be0)
        h = _layer(h, src, dst, norm, n, W1, b1, g1, be1)
        return h

    def _L1_gnn_ref(x, edge_index, edge_attr, W1, b1, W2, b2):
        import jax, jax.numpy as jnp
        import numpy as np
        N_NODES = 50000
        N_EDGES = 12500
        DIM = 96
        src = edge_index[0]
        dst = edge_index[1]
        msg = jax.nn.relu(x[src] + edge_attr)
        aggr = jax.ops.segment_sum(msg, dst, num_segments=x.shape[0])
        h = x + aggr
        h = jax.nn.relu(h @ W1 + b1) @ W2 + b2
        return x + jax.nn.relu(h)
    edge_index = jnp.stack([src, dst])
    h = jnp.maximum(_layernorm(x, axis=-1), 0.0)
    x = x + _L0_gnn_ref(h, edge_index, L0_gnn_W0, L0_gnn_b0, L0_gnn_g0, L0_gnn_be0, L0_gnn_W1, L0_gnn_b1, L0_gnn_g1, L0_gnn_be1)
    h = jnp.maximum(_layernorm(x, axis=-1), 0.0)
    x = x + _L1_gnn_ref(h, edge_index, edge_attr_96, L1_gnn_W1, L1_gnn_b1, L1_gnn_W2, L1_gnn_b2)
    return x

_drawn_inputs = setup_inputs


def setup_inputs(seed=0):
    import zlib

    import numpy as np

    out = dict(_drawn_inputs(seed))
    spreads = {'L0_gnn_b0': (0.0, 0.1),
     'L0_gnn_g0': (1.0, 0.2),
     'L0_gnn_be0': (0.0, 0.1),
     'L0_gnn_b1': (0.0, 0.1),
     'L0_gnn_g1': (1.0, 0.2),
     'L0_gnn_be1': (0.0, 0.1),
     'L1_gnn_b1': (0.0, 0.388),
     'L1_gnn_b2': (0.0, 0.1)}
    factors = {}
    for name, (base, spread) in spreads.items():
        noise = np.random.default_rng([zlib.crc32(name.encode()), seed]).standard_normal(out[name].shape)
        drawn = base * np.exp(spread * noise) if base else spread * noise
        out[name] = jnp.asarray(drawn.astype(out[name].dtype))
    for name, factor in factors.items():
        out[name] = (out[name] * factor).astype(out[name].dtype)
    return out
```

```python
from contextlib import ExitStack

import concourse.bass as bass
from concourse import mybir


def gnn_kernel(nc, x, src, dst, edge_attr, w0, b0, g0, be0, w1, b1, g1, be1, mw1, mb1, mw2, mb2, out):
    fp32, fp16, bf16, i32 = mybir.dt.float32, mybir.dt.float16, mybir.dt.bfloat16, mybir.dt.int32
    ALU = mybir.AluOpType
    ACT = mybir.ActivationFunctionType
    ds = bass.ds

    N, D = x.shape
    E = src.shape[0]
    P, S = 128, 8
    BLOCK = P * S
    BLOCKS = -(-N // BLOCK)
    PADDED = BLOCKS * BLOCK
    TAIL_P = (N - (BLOCKS - 1) * BLOCK) // S
    EP, U = 125, 4
    PER_P = E // EP
    GROUP = EP * U
    GROUPS = PER_P // U
    SPARE = PADDED
    COLS = BLOCKS * S
    HALF = COLS // 2
    EPS = 1e-5
    assert EP * PER_P == E and GROUPS * U == PER_P and TAIL_P * S == N - (BLOCKS - 1) * BLOCK
    assert BLOCKS % 2 == 0 and GROUPS % 2 == 0 and HALF <= 512

    table = nc.dram_tensor("table", (PADDED, D), fp32, kind="Internal").ap()
    accum = nc.dram_tensor("accum", (PADDED + GROUP, D), fp32, kind="Internal").ap()
    skip = nc.dram_tensor("skip", (PADDED, D), fp32, kind="Internal").ap()
    dst_rows = nc.dram_tensor("dst_rows", (GROUPS, GROUP), fp32, kind="Internal").ap()

    def rows(t, blk, parts=P):
        return t[ds(blk * BLOCK, parts * S), :].rearrange("(p s) d -> p (s d)", s=S)

    def steps(eng, count, unroll, base, stages):
        lags = [lag for lag, _ in stages]
        lo, hi = min(lags), max(lags)
        first = 1 - (-hi // unroll)
        last = (count - 1 + lo) // unroll

        def run(turn, at, k0):
            for j in range(unroll):
                for lag, stage in stages:
                    slot, q = (j - lag) % unroll, (j - lag) // unroll
                    if k0 is None:
                        n = at + q if q else at
                        stage(n, slot, n * unroll + (slot - base * unroll))
                    elif 0 <= k0 + j - lag < count:
                        stage(turn + base + q, slot, k0 + j - lag)

        for turn in range(lo // unroll, first):
            run(turn, None, turn * unroll)
        with eng.Fori(base + first, base + last) as at:
            run(None, at, None)
        for turn in range(last, -(-(count + hi) // unroll)):
            run(turn, None, turn * unroll)

    ctx = ExitStack()
    with ctx:
        def sb(name, shape, dt=fp32):
            return ctx.enter_context(nc.sbuf_tensor(name, shape, dt))

        def sbs(name, n, shape, dt=fp32):
            return [sb(f"{name}{i}", shape, dt) for i in range(n)]

        def sem(name):
            return ctx.enter_context(nc.semaphore(name))

        def sems(name, n=2):
            return [sem(f"{name}{i}") for i in range(n)]

        ident = sb("ident", [P, P])
        neg_half = sb("neg_half", [P, 1])
        w0a, w1a, mw2a = (sb(n, [D + 1, D]) for n in ("w0a", "w1a", "mw2a"))
        mw1s = sb("mw1s", [D, D])
        mb1s = sb("mb1s", [D, 1])
        gains = [sb("gain0", [P, D]), sb("gain1", [P, D])]
        shifts = [sb("shift0", [P, D]), sb("shift1", [P, D])]
        dis = sb("dis", [P, COLS])
        deg = sb("deg", [P, COLS])
        src_i = sb("src_i", [EP, PER_P], i32)
        dst_i = sb("dst_i", [EP, PER_P], i32)
        dst_f = sb("dst_f", [EP, PER_P])
        dst_sp = sb("dst_sp", [EP, PER_P])
        row_i = sb("row_i", [EP, PER_P], i32)
        part_i = sb("part_i", [EP, PER_P], i32)
        high_i = sb("high_i", [EP, PER_P], i32)
        low_i = sb("low_i", [EP, PER_P], i32)
        part_f = sb("part_f", [EP, PER_P])
        col_f = sb("col_f", [EP, PER_P])
        count_up = sb("count_up", [EP, COLS], fp16)
        hot = sbs("hot", 2, [EP, U, P + COLS], bf16)
        spare_f = sb("spare_f", [EP, U])
        place = sb("place", [EP, GROUP])
        before = sb("before", [EP, U, GROUP])
        zeros = sb("zeros", [EP, U * D])
        src_slot = sbs("src_slot", 2, [EP, U], i32)
        row_slot = sbs("row_slot", 2, [EP, U], i32)
        dst_row = sbs("dst_row", 2, [P, GROUP])
        same = sbs("same", 2, [EP, U, GROUP])
        junk = sb("junk", [EP, U, GROUP], bf16)
        earlier = sbs("earlier", 2, [EP, U])
        chosen = sbs("chosen", 2, [EP, U])
        got = sbs("got", 2, [EP, U, D])
        attr = sbs("attr", 2, [EP, U, D])
        message = sbs("message", 2, [EP, U, D])
        summed = sbs("summed", 2, [EP, U, D])
        x_in = sbs("x_in", 4, [P, S, D])
        a_in = sbs("a_in", 2, [P, S, D])
        scaled = sbs("scaled", 2, [P, S, D])
        turned = sbs("turned", 2, [D + 1, BLOCK])
        hidden = sbs("hidden", 2, [D + 1, BLOCK])
        tanhs = sbs("tanhs", 2, [P, S, D])
        normed = sbs("normed", 2, [P, S, D])
        gained = sbs("gained", 2, [P, S, D])
        shifted = sbs("shifted", 2, [P, S, D])
        x1 = sbs("x1", 2, [P, S, D])
        h_out = sbs("h_out", 4, [P, S, D])
        x_plus_h = sbs("x_plus_h", 2, [P, S, D])
        stats = sbs("stats", 4, [P, S, 6])
        mean2, mdiff, m2sum, mdiff2, var, rstd, ln_a, ln_b = (
            sbs(n, 4, [P, S]) for n in ("mean2", "mdiff", "m2sum", "mdiff2", "var", "rstd", "ln_a", "ln_b"))
        dis_slot = sbs("dis_slot", 2, [P, S])
        stats2 = sbs("stats2_", 2, [P, S, 6])
        mean2b, mdiffb, m2sumb, mdiff2b, varb, rstdb, ln_a2, ln_b2 = (
            sbs(n, 2, [P, S]) for n in ("mean2b", "mdiffb", "m2sumb", "mdiff2b", "varb", "rstdb", "ln_a2", "ln_b2"))

        ps = [ctx.enter_context(nc.psum_tensor(f"ps{i}", [P, 2, 512], fp32)) for i in range(4)]
        HS = S // 2 * D

        edges_in = sem("edges_in")
        weights_in = sem("weights_in")
        spare_zeroed = sem("spare_zeroed")
        consts_ready = sem("consts_ready")
        fill = sem("fill")
        ones_ready = sem("ones_ready")
        index_ready = sem("index_ready")
        index_step = sem("index_step")
        dst_rows_out = sem("dst_rows_out")
        hot_ready = sems("hot_ready")
        hot_used = sems("hot_used")
        deg_counted = sem("deg_counted")
        deg_ready = sem("deg_ready")
        dis_ready = sem("dis_ready")
        p0_x = sems("p0_x", 4)
        p0_step = sems("p0_step", 4)
        p0_var = sems("p0_var", 4)
        p0_rstd = sems("p0_rstd", 4)
        p0_ab = sems("p0_ab", 4)
        p0_applied = sems("p0_applied", 4)
        p0_stored = sems("p0_stored", 4)
        c_in, c_scaled, c_turned, c_evicted, c_mm, c_tanh = (
            sems(n) for n in ("c_in", "c_scaled", "c_turned", "c_evicted", "c_mm", "c_tanh"))
        c_step, c_var, c_rstd, c_ab, c_applied, c_gained, c_out, c_stored = (
            sems(n) for n in ("c_step", "c_var", "c_rstd", "c_ab", "c_applied", "c_gained", "c_out", "c_stored"))
        d_x, d_shifted, d_x1, d_step, d_var, d_rstd, d_ab, d_skip, d_skip_stored = (
            sems(n) for n in ("d_x", "d_shifted", "d_x1", "d_step", "d_var", "d_rstd", "d_ab", "d_skip", "d_skip_stored"))
        m_in, m_skip, m_turned, m_evicted, m_mm1, m_hidden, m_mm2, m_out, m_stored = (
            sems(n) for n in ("m_in", "m_skip", "m_turned", "m_evicted", "m_mm1", "m_hidden", "m_mm2", "m_out", "m_stored"))
        e_begun = sem("e_begun")
        e_row, e_same, e_rows, e_step, e_src, e_got, e_mm, e_summed, e_added, e_attr, e_msg = (
            sems(n) for n in ("e_row", "e_same", "e_rows", "e_step", "e_src", "e_got", "e_mm", "e_summed",
                              "e_added", "e_attr", "e_msg"))

        BT = BLOCKS // 2
        GT = GROUPS // 2
        P0_USES = [len(range(j, BLOCKS, 4)) for j in range(4)]

        def scatters_done(eng, r):
            for j in range(2):
                eng.wait_ge(e_added[j], 16 * U * GT * (r + 1))

        block = ctx.enter_context(nc.Block())

        @block.sync
        def _(sp):
            sp.dma_start(dst_i[:, :], dst.rearrange("(p c) -> p c", p=EP)).then_inc(edges_in, 16)
            sp.dma_start(src_i[:, :], src.rearrange("(p c) -> p c", p=EP)).then_inc(edges_in, 16)
            for tile, w, b in ((w0a, w0, b0), (w1a, w1, b1), (mw2a, mw2, mb2)):
                sp.dma_start(tile[0:D, :], w).then_inc(weights_in, 16)
                sp.dma_start(tile[D:D + 1, :], b.rearrange("(a d) -> a d", a=1)).then_inc(weights_in, 16)
            sp.dma_start(mw1s[:, :], mw1).then_inc(weights_in, 16)
            sp.dma_start(mb1s[:, :], mb1.rearrange("(d a) -> d a", a=1)).then_inc(weights_in, 16)
            for tile, v in ((gains[0], g0), (gains[1], g1), (shifts[0], be0), (shifts[1], be1)):
                sp.dma_start(tile[:, :], v.rearrange("(a d) -> a d", a=1).to_broadcast([P, D])).then_inc(weights_in, 16)
            sp.wait_ge(consts_ready, 1)
            sp.dma_start(accum[SPARE:SPARE + GROUP, :].rearrange("(p u) d -> p (u d)", u=U),
                         zeros[:, :]).then_inc(spare_zeroed, 16)
            sp.wait_ge(index_step, 1)
            sp.dma_start(dst_rows.rearrange("g (p u) -> p g u", u=U),
                         dst_f[:, :].rearrange("p (g u) -> p g u", u=U)).then_inc(dst_rows_out, 16)

            def load_x0(n, j, blk):
                sp.wait_ge(p0_applied[j], n)
                parts = TAIL_P if isinstance(blk, int) and blk == BLOCKS - 1 else P
                sp.dma_start(x_in[j][0:parts, :, :].rearrange("p s d -> p (s d)"),
                             rows(x, blk, parts)).then_inc(p0_x[j], 16)
            steps(sp, BLOCKS, 4, 0, [(0, load_x0)])

            sp.wait_ge(dst_rows_out, 16)
            for r in range(3):
                def load_row(n, j, g):
                    sp.wait_ge(e_same[j], n)
                    if r == 0:
                        sp.wait_ge(e_rows[j], n)
                    sp.dma_start(dst_row[j][:, :], dst_rows[ds(g, 1), :].to_broadcast([P, GROUP])
                                 ).then_inc(e_row[j], 16)

                def load_attr(n, j, g):
                    sp.wait_ge(e_msg[j], n - 2 * GT)
                    sp.dma_start(attr[j][:, :, :].rearrange("p u d -> p (u d)"),
                                 edge_attr.rearrange("(p c) d -> p (c d)", p=EP)[:, ds(g * (U * D), U * D)]
                                 ).then_inc(e_attr[j], 16)
                steps(sp, GROUPS, 2, r * GT, [(0, load_row)] + ([(0, load_attr)] if r == 2 else []))

                scatters_done(sp, r)
                if r < 2:
                    def load_accum(n, j, blk):
                        sp.wait_ge(c_scaled[j], n)
                        sp.dma_start(a_in[j][:, :, :].rearrange("p s d -> p (s d)"),
                                     rows(accum, blk)).then_inc(c_in[j], 16)

                    def load_x(n, j, blk):
                        sp.wait_ge(d_shifted[j], n - BT)
                        parts = TAIL_P if isinstance(blk, int) and blk == BLOCKS - 1 else P
                        sp.dma_start(x_in[j][0:parts, :, :].rearrange("p s d -> p (s d)"),
                                     rows(x, blk, parts)).then_inc(d_x[j], 16)
                    steps(sp, BLOCKS, 2, r * BT, [(0, load_accum)] + ([(2, load_x)] if r == 1 else []))
                else:
                    for j in range(2):
                        sp.wait_ge(d_skip_stored[j], 16 * BT)

                    def load_last(n, j, blk):
                        sp.wait_ge(m_turned[j], n)
                        sp.dma_start(a_in[j][:, :, :].rearrange("p s d -> p (s d)"),
                                     rows(accum, blk)).then_inc(m_in[j], 16)
                        sp.wait_ge(m_out[j], n)
                        sp.dma_start(x_in[j][:, :, :].rearrange("p s d -> p (s d)"),
                                     rows(skip, blk)).then_inc(m_skip[j], 16)
                    steps(sp, BLOCKS, 2, 0, [(0, load_last)])

        @block.gpsimd
        def _(pool):
            pool.memset(zeros[:, :], 0.0)
            pool.memset(neg_half[:, :], -0.5)
            pool.memset(ident[:, :], 0.0).then_inc(fill, 1)
            pool.iota(count_up[:, :], [[1, COLS]], base=0, channel_multiplier=0, allow_small_or_imprecise_dtypes=True)
            pool.iota(place[:, :], [[1, GROUP]], base=0, channel_multiplier=-U, allow_small_or_imprecise_dtypes=True)
            pool.iota(spare_f[:, :], [[EP, U]], base=SPARE, channel_multiplier=1, allow_small_or_imprecise_dtypes=True)
            pool.wait_ge(fill, 1)
            pool.affine_select(out=ident[:, :], in_=ident[:, :], compare_op=ALU.not_equal, fill=1.0,
                               base=0, pattern=[[-1, P]], channel_multiplier=1).then_inc(consts_ready, 1)
            pool.wait_ge(deg_ready, 1)
            pool.tensor_tensor(dis[:, :], deg[:, :], neg_half[:, :].to_broadcast([P, COLS]), ALU.pow
                               ).then_inc(dis_ready, 1)

            def power(var_ready, var_t, rstd_t, rstd_ready):
                def stage(n, j, blk):
                    pool.wait_ge(var_ready[j], n + 1)
                    pool.tensor_tensor(rstd_t[j][:, :], var_t[j][:, :], neg_half[:, :].to_broadcast([P, S]),
                                       ALU.pow).then_inc(rstd_ready[j], 1)
                return stage

            steps(pool, BLOCKS, 4, 0, [(0, power(p0_var, var, rstd, p0_rstd))])

            for r in range(3):
                if r == 0:
                    pool.wait_ge(spare_zeroed, 16)
                    for j in range(4):
                        pool.wait_ge(p0_stored[j], 32 * P0_USES[j])
                else:
                    for j in range(2):
                        pool.wait_ge(c_stored[j], 32 * BT * r)

                def scatter(n, j, g):
                    pool.wait_ge(e_summed[j], n + 1)
                    pool.wait_ge(e_rows[j], n + 1)
                    pool.wait_ge(e_added[1 - j], 16 * U * (n + j))
                    pool.sem_inc(e_begun, 1)
                    for u in range(U):
                        pool.indirect_dma_start(
                            out=accum[:, :], out_offset=bass.IndirectOffsetOnAxis(ap=row_slot[j][:, u:u + 1], axis=0),
                            in_=summed[j][:, u, :], in_offset=None, compute_op=ALU.add).then_inc(e_added[j], 16)

                def gather(n, j, g):
                    pool.wait_ge(e_src[j], n + 1)
                    pool.sem_inc(e_begun, 1)
                    for u in range(U):
                        pool.indirect_dma_start(
                            out=got[j][:, u, :], out_offset=None, in_=table[:, :],
                            in_offset=bass.IndirectOffsetOnAxis(ap=src_slot[j][:, u:u + 1], axis=0)
                        ).then_inc(e_got[j], 16)
                steps(pool, GROUPS, 2, r * GT, [(0, scatter), (-2, gather)])

                if r == 2:
                    continue
                last_pass = r == 1

                def gain(n, j, blk):
                    pool.wait_ge(c_applied[j], n + 1)
                    pool.wait_ge(c_out[j], n)
                    pool.tensor_tensor(gained[j][:, :, :], normed[j][:, :, :],
                                       gains[r][:, :].unsqueeze(1).to_broadcast([P, S, D]), ALU.mult
                                       ).then_inc(c_gained[j], 1)

                def shift_x(n, j, blk):
                    pool.wait_ge(d_x[j], 16 * (n + 1 - BT))
                    pool.wait_ge(c_out[j], n)
                    pool.tensor_tensor(shifted[j][:, :, :], x_in[j][:, :, :],
                                       shifts[1][:, :].unsqueeze(1).to_broadcast([P, S, D]), ALU.add
                                       ).then_inc(d_shifted[j], 1)

                def add_skip(n, j, blk):
                    pool.wait_ge(d_x1[j], n + 1 - BT)
                    pool.wait_ge(d_skip_stored[j], 16 * (n - BT))
                    pool.tensor_tensor(x_plus_h[j][:, :, :], x1[j][:, :, :], h_out[j][:, :, :], ALU.add
                                       ).then_inc(d_skip[j], 1)

                def power_d(n, j, blk):
                    pool.wait_ge(d_var[j], n + 1 - BT)
                    pool.tensor_tensor(rstdb[j][:, :], varb[j][:, :], neg_half[:, :].to_broadcast([P, S]),
                                       ALU.pow).then_inc(d_rstd[j], 1)
                if last_pass:
                    stages = [(4, add_skip), (0, power(c_var, var, rstd, c_rstd)), (1, gain), (1, shift_x), (2, power_d)]
                else:
                    stages = [(0, power(c_var, var, rstd, c_rstd)), (1, gain)]
                steps(pool, BLOCKS, 2, r * BT, stages)

        @block.vector
        def _(dve):
            for j in range(2):
                dve.memset(turned[j][D:D + 1, :], 1.0)
                dve.memset(hidden[j][D:D + 1, :], 1.0).then_inc(ones_ready, 1)
            dve.wait_ge(edges_in, 32)
            dve.tensor_copy(dst_f[:, :], dst_i[:, :]).then_inc(index_step, 1)
            dve.tensor_scalar(part_i[:, :], dst_i[:, :], 3, P - 1, ALU.arith_shift_right, ALU.bitwise_and)
            dve.tensor_scalar(high_i[:, :], dst_i[:, :], 10, 3, ALU.arith_shift_right, ALU.logical_shift_left)
            dve.tensor_scalar(low_i[:, :], dst_i[:, :], S - 1, None, ALU.bitwise_and).then_inc(index_step, 1)
            dve.wait_ge(index_step, 2)
            dve.tensor_copy(part_f[:, :], part_i[:, :])
            dve.tensor_tensor(col_f[:, :], high_i[:, :], low_i[:, :], ALU.add).then_inc(index_step, 1)
            dve.wait_ge(consts_ready, 1)
            dve.tensor_tensor(dst_sp[:, :].rearrange("p (g u) -> p g u", u=U),
                              dst_f[:, :].rearrange("p (g u) -> p g u", u=U),
                              spare_f[:, :].unsqueeze(1).to_broadcast([EP, GROUPS, U]), ALU.subtract)
            for u in range(U):
                dve.tensor_scalar(before[:, u, :], place[:, :], float(u), None, ALU.is_lt).then_inc(index_ready, 1)
            dve.wait_ge(index_step, 3)

            def one_hot(n, j, g):
                dve.wait_ge(hot_used[j], n)
                for u in range(U):
                    dve.tensor_scalar(hot[j][:, u, 0:P], count_up[:, 0:P], part_f[:, ds(g * U + u, 1)], None,
                                      ALU.is_equal)
                    last = dve.tensor_scalar(hot[j][:, u, P:P + COLS], count_up[:, :], col_f[:, ds(g * U + u, 1)],
                                             None, ALU.is_equal)
                last.then_inc(hot_ready[j], 1)
            steps(dve, GROUPS, 2, 0, [(0, one_hot)])
            dve.wait_ge(deg_counted, 1)
            dve.tensor_scalar(deg[:, :].rearrange("p (h c) -> p h c", h=2), ps[0][:, :, 0:HALF], 1.0, None,
                              ALU.add).then_inc(deg_ready, 1)

            def variance(st, m2, md, ms, md2, va, step, waits, src_t, var_ready):
                def stage(n, j, blk, k=0):
                    s = step[j]
                    for i in range(S):
                        last = dve.bn_stats(st[j][:, i, :], src_t[j][:, i, :])
                    last.then_inc(s, 1)
                    dve.wait_ge(s, 3 * (n - k) + 1)
                    dve.tensor_tensor(m2[j][:, :], st[j][:, :, 1], st[j][:, :, 4], ALU.add)
                    dve.scalar_tensor_tensor(out=ms[j][:, :], in0=st[j][:, :, 2], scalar=EPS * D,
                                             in1=st[j][:, :, 5], op0=ALU.add, op1=ALU.add)
                    dve.tensor_tensor(md[j][:, :], st[j][:, :, 1], st[j][:, :, 4], ALU.subtract).then_inc(s, 1)
                    dve.wait_ge(s, 3 * (n - k) + 2)
                    dve.scalar_tensor_tensor(out=md2[j][:, :], in0=md[j][:, :], scalar=0.25, in1=md[j][:, :],
                                             op0=ALU.mult, op1=ALU.mult).then_inc(s, 1)
                    dve.wait_ge(s, 3 * (n - k) + 3)
                    dve.scalar_tensor_tensor(out=va[j][:, :], in0=ms[j][:, :], scalar=1.0 / D, in1=md2[j][:, :],
                                             op0=ALU.mult, op1=ALU.add).then_inc(var_ready[j], 1)
                return stage

            var0 = variance(stats, mean2, mdiff, m2sum, mdiff2, var, p0_step, None, x_in, p0_var)

            def stats0(n, j, blk):
                dve.wait_ge(p0_x[j], 16 * (n + 1))
                var0(n, j, blk)

            def scales0(n, j, blk):
                dve.wait_ge(p0_rstd[j], n + 1)
                dve.wait_ge(p0_applied[j], n)
                dve.tensor_tensor(ln_a[j][:, :], rstd[j][:, :], dis[:, ds(blk * S, S)], ALU.mult
                                  ).then_inc(p0_ab[j], 1)
                dve.wait_ge(p0_ab[j], 2 * n + 1)
                dve.scalar_tensor_tensor(out=ln_b[j][:, :], in0=mean2[j][:, :], scalar=-0.5, in1=ln_a[j][:, :],
                                         op0=ALU.mult, op1=ALU.mult).then_inc(p0_ab[j], 1)
            dve.wait_ge(dis_ready, 1)
            steps(dve, BLOCKS, 4, 0, [(0, stats0), (1, scales0)])

            dve.wait_ge(index_ready, U)
            for r in range(3):
                def compare(n, j, g):
                    dve.wait_ge(e_row[j], 16 * (n + 1))
                    dve.wait_ge(e_mm[j], n)
                    for u in range(U):
                        last = dve.tensor_scalar(same[j][:, u, :], dst_row[j][0:EP, :], dst_f[:, ds(g * U + u, 1)],
                                                 None, ALU.is_equal)
                    last.then_inc(e_same[j], 1)

                def choose(n, j, g):
                    for u in range(U):
                        last = dve.scalar_tensor_tensor(
                            out=junk[:, u, :], in0=dst_row[j][0:EP, :], scalar=dst_f[:, ds(g * U + u, 1)],
                            in1=before[:, u, :], op0=ALU.is_equal, op1=ALU.mult, accum_out=earlier[j][:, u:u + 1])
                    last.then_inc(e_step[j], 1)
                    dve.wait_ge(e_step[j], 3 * n + 1)
                    dve.scalar_tensor_tensor(out=chosen[j][:, :], in0=earlier[j][:, :], scalar=0.0,
                                             in1=dst_sp[:, ds(g * U, U)], op0=ALU.is_equal, op1=ALU.mult
                                             ).then_inc(e_step[j], 1)
                    dve.wait_ge(e_step[j], 3 * n + 2)
                    dve.tensor_tensor(row_i[:, ds(g * U, U)], chosen[j][:, :], spare_f[:, :], ALU.add
                                      ).then_inc(e_step[j], 1)
                    dve.wait_ge(e_step[j], 3 * n + 3)

                def take_rows(n, j, g):
                    dve.wait_ge(e_added[j], 16 * U * n)
                    dve.tensor_scalar(row_slot[j][:, :], row_i[:, ds(g * U, U)], 0.0, None, ALU.add).then_inc(e_rows[j], 1)

                def add_attr(n, j, g):
                    dve.wait_ge(e_got[j], 16 * U * (n + 1))
                    dve.wait_ge(e_attr[j], 16 * (n + 1 - 2 * GT))
                    dve.tensor_tensor(message[j][:, :, :], got[j][:, :, :], attr[j][:, :, :], ALU.add
                                      ).then_inc(e_step[j], 1)
                    dve.wait_ge(e_step[j], n + 1 + GT)
                    dve.tensor_scalar(message[j][:, :, :], message[j][:, :, :], 0.0, None, ALU.max
                                      ).then_inc(e_msg[j], 1)
                stages = [(0, compare)]
                if r == 0:
                    stages.append((0, choose))
                stages.append((0, take_rows))
                if r == 2:
                    stages.append((0, add_attr))
                steps(dve, GROUPS, 2, r * GT, stages)

                if r == 2:
                    continue
                last_pass = r == 1

                def scale(n, j, blk):
                    dve.wait_ge(c_in[j], 16 * (n + 1))
                    dve.wait_ge(c_turned[j], n)
                    dve.tensor_tensor(scaled[j][:, :, :], a_in[j][:, :, :],
                                      dis[:, ds(blk * S, S)].unsqueeze(2).to_broadcast([P, S, D]), ALU.mult
                                      ).then_inc(c_scaled[j], 1)
                var1 = variance(stats, mean2, mdiff, m2sum, mdiff2, var, c_step, None, tanhs, c_var)

                def stats1(n, j, blk):
                    dve.wait_ge(c_tanh[j], n + 1)
                    var1(n, j, blk)

                def scales1(n, j, blk):
                    dve.wait_ge(c_rstd[j], n + 1)
                    dve.wait_ge(c_applied[j], n)
                    if last_pass:
                        dve.tensor_copy(ln_a[j][:, :], rstd[j][:, :]).then_inc(c_ab[j], 1)
                    else:
                        dve.wait_ge(c_out[j], n)
                        dve.tensor_scalar(dis_slot[j][:, :], dis[:, ds(blk * S, S)], 1.0, None, ALU.mult)
                        dve.tensor_tensor(ln_a[j][:, :], rstd[j][:, :], dis[:, ds(blk * S, S)], ALU.mult
                                          ).then_inc(c_ab[j], 1)
                    dve.wait_ge(c_ab[j], 2 * n + 1)
                    dve.scalar_tensor_tensor(out=ln_b[j][:, :], in0=mean2[j][:, :], scalar=-0.5, in1=ln_a[j][:, :],
                                             op0=ALU.mult, op1=ALU.mult).then_inc(c_ab[j], 1)

                def add_shift(n, j, blk):
                    dve.wait_ge(c_gained[j], n + 1)
                    dve.wait_ge(c_stored[j], 32 * n)
                    for i in range(S):
                        last = dve.scalar_tensor_tensor(out=h_out[j][:, i, :], in0=shifts[0][:, :],
                                                        scalar=dis_slot[j][:, i:i + 1], in1=gained[j][:, i, :],
                                                        op0=ALU.mult, op1=ALU.add)
                    last.then_inc(c_out[j], 1)

                var2 = variance(stats2, mean2b, mdiffb, m2sumb, mdiff2b, varb, d_step, None, x1, d_var)

                def residual(n, j, blk):
                    dve.wait_ge(c_gained[j], n + 1)
                    dve.wait_ge(d_shifted[j], n + 1 - BT)
                    dve.wait_ge(d_skip[j], n - BT)
                    dve.tensor_tensor(x1[j][:, :, :], gained[j][:, :, :], shifted[j][:, :, :], ALU.add
                                      ).then_inc(c_out[j], 1)
                    dve.wait_ge(c_out[j], n + 1)
                    var2(n, j, blk, k=BT)

                def scales2(n, j, blk):
                    dve.wait_ge(d_rstd[j], n + 1 - BT)
                    dve.wait_ge(d_x1[j], n - BT)
                    dve.tensor_copy(ln_a2[j][:, :], rstdb[j][:, :])
                    dve.scalar_tensor_tensor(out=ln_b2[j][:, :], in0=mean2b[j][:, :], scalar=-0.5,
                                             in1=rstdb[j][:, :], op0=ALU.mult, op1=ALU.mult).then_inc(d_ab[j], 1)
                if last_pass:
                    stages = [(-2, scale), (1, scales1), (0, stats1), (3, scales2), (2, residual)]
                else:
                    stages = [(-2, scale), (1, scales1), (0, stats1), (2, add_shift)]
                steps(dve, BLOCKS, 2, r * BT, stages)

            def finish(n, j, blk):
                dve.wait_ge(m_mm2[j], n + 1)
                dve.wait_ge(m_skip[j], 16 * (n + 1))
                dve.wait_ge(m_stored[j], 16 * n)
                dve.scalar_tensor_tensor(out=h_out[j][:, :, :].rearrange("p (h s) d -> p h (s d)", h=2),
                                         in0=ps[2 + j][:, :, 0:HS], scalar=0.0,
                                         in1=x_in[j][:, :, :].rearrange("p (h s) d -> p h (s d)", h=2),
                                         op0=ALU.max, op1=ALU.add).then_inc(m_out[j], 1)
            steps(dve, BLOCKS, 2, 0, [(0, finish)])

        @block.scalar
        def _(act):
            def apply0(n, j, blk):
                act.wait_ge(p0_ab[j], 2 * n + 2)
                act.wait_ge(p0_stored[j], 32 * n)
                for i in range(S):
                    last = act.activation(h_out[j][:, i, :], x_in[j][:, i, :], ACT.Relu,
                                          bias=ln_b[j][:, i:i + 1], scale=ln_a[j][:, i:i + 1])
                last.then_inc(p0_applied[j], 1)

            def store0(n, j, blk):
                act.wait_ge(p0_applied[j], n + 1)
                for t in (table, accum):
                    act.dma_start(rows(t, blk), h_out[j][:, :, :].rearrange("p s d -> p (s d)")
                                  ).then_inc(p0_stored[j], 16)
            steps(act, BLOCKS, 4, 0, [(2, store0), (1, apply0)])

            for r in range(3):
                def take_src(n, j, g):
                    act.wait_ge(e_mm[j], n)
                    act.copy(src_slot[j][:, :], src_i[:, ds(g * U, U)]).then_inc(e_src[j], 1)

                def evict_sums(n, j, g):
                    act.wait_ge(e_mm[j], n + 1)
                    act.wait_ge(e_added[j], 16 * U * n)
                    act.copy(summed[j][:, :, :].rearrange("p u d -> p (u d)"), ps[j][0:EP, 0, 0:U * D]
                             ).then_inc(e_summed[j], 1)
                steps(act, GROUPS, 2, r * GT, [(-2, take_src), (0, evict_sums)])

                if r == 2:
                    continue
                last_pass = r == 1

                def evict(n, j, blk):
                    act.wait_ge(c_turned[j], n + 1)
                    act.wait_ge(c_mm[j], n)
                    act.copy(turned[j][0:D, :].rearrange("p (h c) -> p h c", h=2), ps[j][0:D, :, :]
                             ).then_inc(c_evicted[j], 1)

                def tanh(n, j, blk):
                    act.wait_ge(c_mm[j], n + 1)
                    act.wait_ge(c_applied[j], n)
                    act.activation(tanhs[j][:, :, :].rearrange("p (h s) d -> p h (s d)", h=2),
                                   ps[2 + j][:, :, 0:HS], ACT.Tanh).then_inc(c_tanh[j], 1)

                def apply(n, j, blk):
                    act.wait_ge(c_ab[j], 2 * n + 2)
                    act.wait_ge(c_gained[j], n)
                    for i in range(S):
                        last = act.activation(normed[j][:, i, :], tanhs[j][:, i, :], ACT.Identity,
                                              bias=ln_b[j][:, i:i + 1], scale=ln_a[j][:, i:i + 1])
                    last.then_inc(c_applied[j], 1)

                def apply2(n, j, blk):
                    act.wait_ge(d_ab[j], n + 1 - BT)
                    act.wait_ge(c_stored[j], 32 * n)
                    act.wait_ge(d_skip[j], n - BT)
                    for i in range(S):
                        last = act.activation(h_out[j][:, i, :], x1[j][:, i, :], ACT.Relu,
                                              bias=ln_b2[j][:, i:i + 1], scale=ln_a2[j][:, i:i + 1])
                    last.then_inc(d_x1[j], 1)

                def store(n, j, blk):
                    if last_pass:
                        act.wait_ge(d_x1[j], n + 1 - BT)
                    else:
                        act.wait_ge(c_out[j], n + 1)
                    for t in (table, accum):
                        act.dma_start(rows(t, blk), h_out[j][:, :, :].rearrange("p s d -> p (s d)")
                                      ).then_inc(c_stored[j], 16)

                def store_skip(n, j, blk):
                    act.wait_ge(d_skip[j], n + 1 - BT)
                    act.dma_start(rows(skip, blk), x_plus_h[j][:, :, :].rearrange("p s d -> p (s d)")
                                  ).then_inc(d_skip_stored[j], 16)
                if last_pass:
                    stages = [(4, store), (5, store_skip), (-1, evict), (0, tanh), (1, apply), (3, apply2)]
                else:
                    stages = [(3, store), (-1, evict), (0, tanh), (1, apply)]
                steps(act, BLOCKS, 2, r * BT, stages)

            def evict_last(n, j, blk):
                act.wait_ge(m_turned[j], n + 1)
                act.wait_ge(m_mm1[j], n)
                act.copy(turned[j][0:D, :].rearrange("p (h c) -> p h c", h=2), ps[0][0:D, :, :]
                         ).then_inc(m_evicted[j], 1)

            def hide(n, j, blk):
                act.wait_ge(m_mm1[j], n + 1)
                act.wait_ge(m_mm2[j], n)
                act.activation(hidden[j][0:D, :].rearrange("p (h c) -> p h c", h=2), ps[1][0:D, :, :],
                               ACT.Relu, bias=mb1s[:, :]).then_inc(m_hidden[j], 1)

            def store_out(n, j, blk):
                act.wait_ge(m_out[j], n + 1)
                parts = TAIL_P if isinstance(blk, int) and blk == BLOCKS - 1 else P
                act.dma_start(rows(out, blk, parts), h_out[j][0:parts, :, :].rearrange("p s d -> p (s d)")
                              ).then_inc(m_stored[j], 16)
            steps(act, BLOCKS, 2, 0, [(2, store_out), (0, hide), (-1, evict_last)])
            for j in range(2):
                act.wait_ge(m_stored[j], 16 * BT)

        @block.tensor
        def _(pe):
            def count(n, j, g):
                pe.wait_ge(hot_ready[j], n + 1)
                for u in range(U):
                    for h in range(2):
                        last = pe.matmul(ps[0][:, h, 0:HALF], hot[j][:, u, 0:P],
                                         hot[j][:, u, P + h * HALF:P + (h + 1) * HALF],
                                         start=isinstance(g, int) and g == 0 and u == 0,
                                         stop=isinstance(g, int) and g == GROUPS - 1 and u == U - 1)
                last.then_inc(hot_used[j], 1)
                if isinstance(g, int) and g == GROUPS - 1:
                    pe.wait_ge(hot_used[j], n + 1)
                    pe.sem_inc(deg_counted, 1)
            steps(pe, GROUPS, 2, 0, [(0, count)])

            pe.wait_ge(weights_in, 16 * 12)
            pe.wait_ge(ones_ready, 2)
            pe.wait_ge(consts_ready, 1)
            for r in range(3):
                def sums(n, j, g):
                    pe.wait_ge(e_same[j], n + 1)
                    if r == 2:
                        pe.wait_ge(e_msg[j], n + 1 - 2 * GT)
                        rhs = message
                    else:
                        pe.wait_ge(e_got[j], 16 * U * (n + 1))
                        rhs = got
                    pe.wait_ge(e_summed[j], n)
                    for i in range(U):
                        for u in range(U):
                            last = pe.matmul(ps[j][0:EP, 0, i * D:(i + 1) * D],
                                             same[j][:, u, :].rearrange("p (q i) -> p i q", i=U)[:, i, :],
                                             rhs[j][:, u, :], start=u == 0, stop=u == U - 1)
                    last.then_inc(e_mm[j], 1)
                steps(pe, GROUPS, 2, r * GT, [(0, sums)])

                if r == 2:
                    continue
                wa = (w0a, w1a)[r]

                def turn(n, j, blk):
                    pe.wait_ge(c_scaled[j], n + 1)
                    pe.wait_ge(c_evicted[j], n)
                    for i in range(S):
                        last = pe.transpose(ps[j][0:D, i // 4, (i % 4) * P:(i % 4 + 1) * P],
                                            scaled[j][:, i, :], ident[:, :])
                    last.then_inc(c_turned[j], 1)

                def project(n, j, blk):
                    pe.wait_ge(c_evicted[j], n + 1)
                    pe.wait_ge(c_tanh[j], n)
                    for i in range(S):
                        last = pe.matmul(ps[2 + j][:, i // 4, (i % 4) * D:(i % 4 + 1) * D],
                                         turned[j][:, i * P:(i + 1) * P], wa[:, :], start=True, stop=True)
                    last.then_inc(c_mm[j], 1)
                steps(pe, BLOCKS, 2, r * BT, [(-1, turn), (0, project)])

            def hide_mm(n, j, blk):
                pe.wait_ge(m_evicted[j], n + 1)
                pe.wait_ge(m_hidden[1 - j], n + j)
                for h in range(2):
                    last = pe.matmul(ps[1][0:D, h, :], mw1s[:, :], turned[j][0:D, h * 512:(h + 1) * 512],
                                     start=True, stop=True)
                last.then_inc(m_mm1[j], 1)

            def turn_last(n, j, blk):
                pe.wait_ge(m_in[j], 16 * (n + 1))
                pe.wait_ge(m_evicted[1 - j], n + j)
                for i in range(S):
                    last = pe.transpose(ps[0][0:D, i // 4, (i % 4) * P:(i % 4 + 1) * P],
                                        a_in[j][:, i, :], ident[:, :])
                last.then_inc(m_turned[j], 1)

            def project_last(n, j, blk):
                pe.wait_ge(m_hidden[j], n + 1)
                pe.wait_ge(m_out[j], n)
                for i in range(S):
                    last = pe.matmul(ps[2 + j][:, i // 4, (i % 4) * D:(i % 4 + 1) * D],
                                     hidden[j][:, i * P:(i + 1) * P], mw2a[:, :], start=True, stop=True)
                last.then_inc(m_mm2[j], 1)
            steps(pe, BLOCKS, 2, 0, [(0, hide_mm), (-1, turn_last), (0, project_last)])


_INS = ['x', 'src', 'dst', 'edge_attr_96', 'L0_gnn_W0', 'L0_gnn_b0', 'L0_gnn_g0', 'L0_gnn_be0', 'L0_gnn_W1',
        'L0_gnn_b1', 'L0_gnn_g1', 'L0_gnn_be1', 'L1_gnn_W1', 'L1_gnn_b1', 'L1_gnn_W2', 'L1_gnn_b2']


def kernel(**inputs):
    import numpy as np
    import concourse.bacc as bacc
    from concourse.bass_utils import run_bass_kernel_spmd

    nc = bacc.Bacc("TRN2", target_bir_lowering=False, num_devices=1)
    arrays, args = {}, []
    for name in _INS:
        a = np.ascontiguousarray(inputs[name])
        arrays[f"in_{name}"] = a
        args.append(nc.dram_tensor(f"in_{name}", a.shape, mybir.dt.from_np(a.dtype), kind="ExternalInput").ap())
    x = inputs["x"]
    args.append(nc.dram_tensor("out_0", x.shape, mybir.dt.float32, kind="ExternalOutput").ap())
    gnn_kernel(nc, *args)
    return run_bass_kernel_spmd(nc, [arrays], core_ids=[0]).results[0]["out_0"]
```

```python
from contextlib import ExitStack

import concourse.bass as bass
from concourse import mybir


class Item:

    def __init__(self, at, per, c, total):
        self.at, self.per, self.c, self.total = at, per, c, total
        self.index = c if at is None else at * per + c

    def of(self, ring, passes=0):
        slot = self.c % ring
        n = self.c // ring + passes * len(range(slot, self.total, ring))
        if self.at is not None:
            n = self.at * (self.per // ring) + n if self.per != ring else self.at + n
        return slot, n

    def last(self):
        return self.at is None and self.c == self.total - 1


def run_steps(eng, per_turn, stages):
    def events(turn):
        found = []
        for order, (lag, stage, items, total, lo, hi) in enumerate(stages):
            for j in range(items):
                i = turn * items + j - lag
                if lo <= i < hi:
                    found.append((j / items, order, i, i < 4 or i == total - 1))
        return sorted(found)

    def run(turn, at):
        for _, order, i, _ in events(turn):
            lag, stage, items, total, lo, hi = stages[order]
            if at is None:
                stage(Item(None, items, i, total))
            else:
                stage(Item(at, items, i - turn * items, total))

    first = min((s[0] + s[4]) // s[2] for s in stages)
    end = max(-(-(s[0] + s[5]) // s[2]) for s in stages)
    kinds = [([(p, o) for p, o, _, _ in events(t)], any(e[3] for e in events(t))) for t in range(first, end)]
    t = first
    while t < end:
        stretch = 1
        while t + stretch < end and not kinds[t - first][1] and kinds[t + stretch - first] == kinds[t - first]:
            stretch += 1
        if stretch >= 3 and t > 0:
            with eng.Fori(t, t + stretch) as at:
                run_at_loop(stages, events(t), t, at)
        else:
            for s in range(t, t + stretch):
                run(s, None)
        t += stretch


def run_at_loop(stages, found, turn, at):
    for _, order, i, _ in found:
        lag, stage, items, total, lo, hi = stages[order]
        stage(Item(at, items, i - turn * items, total))


def gnn_kernel(nc, x, src, dst, edge_attr, w0, b0, g0, be0, w1, b1, g1, be1, mw1, mb1, mw2, mb2, out):
    fp32, fp16, bf16, i32 = mybir.dt.float32, mybir.dt.float16, mybir.dt.bfloat16, mybir.dt.int32
    ALU = mybir.AluOpType
    ACT = mybir.ActivationFunctionType
    AX = mybir.AxisListType
    ds = bass.ds

    N, D = x.shape
    E = src.shape[0]
    P, S = 128, 8
    BLOCK = P * S
    BLOCKS = -(-N // BLOCK)
    PADDED = BLOCKS * BLOCK
    TAIL_P = (N - (BLOCKS - 1) * BLOCK) // S
    U = 4
    GROUP = P * U
    GROUPS = -(-E // GROUP)
    PER_P = GROUPS * U
    TAIL_E = (E - (GROUPS - 1) * GROUP) // U
    WIDE = D + 1
    SPARE = PADDED
    COLS = BLOCKS * S
    HALF = COLS // 2
    EPS = 1e-5
    HS = S // 2 * D
    HB = BLOCK // 2
    LEAD = 26
    assert TAIL_P * S == N - (BLOCKS - 1) * BLOCK and TAIL_E * U == E - (GROUPS - 1) * GROUP
    assert HALF <= 512 and U * WIDE <= 512 and LEAD % 2 == 0 and LEAD < GROUPS

    table_d, table_w = (nc.dram_tensor(n, (PADDED, w), fp32, kind="Internal").ap()
                        for n, w in (("table_d", D), ("table_w", WIDE)))
    accum_d, accum_w = (nc.dram_tensor(n, (PADDED + GROUP, w), fp32, kind="Internal").ap()
                        for n, w in (("accum_d", D), ("accum_w", WIDE)))
    tables, accums, widths = (table_d, table_w, table_d), (accum_d, accum_w, accum_d), (D, WIDE, D)
    skip = nc.dram_tensor("skip", (PADDED, D), fp32, kind="Internal").ap()

    def rows(t, blk, parts=P):
        return t[ds(blk * BLOCK, parts * S), :].rearrange("(p s) d -> p (s d)", s=S)

    def wide(t, w):
        return t[:, 0:S * w].rearrange("p (s d) -> p s d", s=S)

    def row(v):
        return v.rearrange("(a d) -> a d", a=1)

    def block_parts(it):
        return TAIL_P if it.last() else P

    def edge_parts(it):
        return TAIL_E if it.last() else P

    def groups(lag, stage):
        return (lag, stage, 4, GROUPS, 0, GROUPS)

    def blocks(lag, stage, lo=0, hi=BLOCKS):
        return (lag, stage, 4, BLOCKS, max(lo, 0), max(hi, 0))

    def halves(lag, stage):
        return (lag, stage, 8, 2 * BLOCKS, 0, 2 * BLOCKS)

    def half(it):
        h, n = it.of(2)
        return it.c // 2 % 2, h, n

    def four_back(it):
        return it.at is not None or it.c >= 4

    ctx = ExitStack()
    with ctx:
        def sb(name, shape, dt=fp32):
            return ctx.enter_context(nc.sbuf_tensor(name, shape, dt))

        def sbs(name, n, shape, dt=fp32):
            return [sb(f"{name}{i}_", shape, dt) for i in range(n)]

        def sem(name):
            return ctx.enter_context(nc.semaphore(name))

        def sems(name, n):
            return [sem(f"{name}{i}") for i in range(n)]

        ident = sb("ident", [P, P])
        neg_half = sb("neg_half", [P, 1])
        w0a, mw2a = (sb(n, [D + 1, D]) for n in ("w0a", "mw2a"))
        w1a = sb("w1a", [D + 2, D])
        w1s = sb("w1s", [D, D])
        g0c, be0c = sb("g0c", [D, 1]), sb("be0c", [D, 1])
        mw1s = sb("mw1s", [D, D])
        mb1s = sb("mb1s", [D, 1])
        gain1, shift1 = sb("gain1", [P, D]), sb("shift1", [P, D])
        dis = sb("dis", [P, COLS])
        deg = sb("deg", [P, COLS])
        newton = sb("newton", [P, COLS])
        src_i = sb("src_i", [P, PER_P], i32)
        dst_i = sb("dst_i", [P, PER_P], i32)
        dst_f = sb("dst_f", [P, PER_P])
        dst_sp = sb("dst_sp", [P, PER_P])
        row_i = sb("row_i", [P, PER_P], i32)
        part_i = sb("part_i", [P, PER_P], i32)
        high_i = sb("high_i", [P, PER_P], i32)
        low_i = sb("low_i", [P, PER_P], i32)
        part_f = sb("part_f", [P, PER_P])
        col_f = sb("col_f", [P, PER_P])
        earliest = sb("earliest", [P, GROUPS, U])
        slack = sb("slack", [P, PER_P])
        least = sb("least", [P, 1])
        least_all = sb("least_all", [1, 1])
        ahead = sb("ahead", [1, 1], i32)
        count_up = sb("count_up", [P, COLS], fp16)
        part_slot = sbs("part_slot", 2, [P, U])
        hot_part = sbs("hot_part", 2, [P, U, P], bf16)
        hot_col = sbs("hot_col", 2, [P, U, COLS], bf16)
        spare_f = sb("spare_f", [P, U])
        place = sb("place", [P, GROUP])
        before = sb("before", [P, U, GROUP], bf16)
        zeros = sb("zeros", [P, U * WIDE])
        src_slot = sbs("src_slot", 4, [P, U], i32)
        row_slot = sbs("row_slot", 2, [P, U], i32)
        dst_row = sbs("dst_row", 2, [P, GROUP], i32)
        same = sbs("same", 2, [P, U, GROUP])
        junk = sb("junk", [P, U, GROUP], bf16)
        earlier = sbs("earlier", 2, [P, U])
        chosen = sbs("chosen", 2, [P, U])
        got = sbs("got", 4, [P, U, WIDE])
        attr = sbs("attr", 2, [P, U, D])
        message = sbs("message", 2, [P, U, D])
        summed = sbs("summed", 2, [P, U, WIDE])
        x_in = sbs("x_in", 4, [P, S, D])
        a_in = sbs("a_in", 2, [P, S * WIDE])
        scaled = sbs("scaled", 2, [P, S * WIDE])
        turned = sbs("turned", 2, [D + 2, BLOCK])
        hidden = sbs("hidden", 2, [D + 1, BLOCK])
        tanhs = sbs("tanhs", 4, [P, S, D])
        normed = sbs("normed", 2, [P, S, D])
        gained = sbs("gained", 2, [P, S, D])
        shifted = sbs("shifted", 2, [P, S, D])
        x1 = sbs("x1", 4, [P, S, D])
        h_out = sbs("h_out", 4, [P, S * WIDE])
        x_plus_h = sbs("x_plus_h", 2, [P, S, D])
        stats = sbs("stats", 4, [P, S, 6])
        mean2, mdiff, m2sum, mdiff2, var, rstd, ln_a, ln_b = (
            sbs(n, 4, [P, S]) for n in ("mean2", "mdiff", "m2sum", "mdiff2", "var", "rstd", "ln_a", "ln_b"))
        stats_b = sbs("stats_b", 4, [P, S, 6])
        mean2_b, mdiff_b, m2sum_b, mdiff2_b, var_b, rstd_b, ln_b_b = (
            sbs(n + "_b", 4, [P, S]) for n in ("mean2", "mdiff", "m2sum", "mdiff2", "var", "rstd", "ln_b"))

        ps = [ctx.enter_context(nc.psum_tensor(f"ps{i}", [P, 2, 512], fp32)) for i in range(4)]
        ps_turn, ps_sum, ps_out = ps[0], ps[1], (ps[2], ps[3])

        edges_in = sem("edges_in")
        weights_in = sem("weights_in")
        spare_zeroed = sem("spare_zeroed")
        consts_ready = sem("consts_ready")
        fill = sem("fill")
        ones_ready = sem("ones_ready")
        index_ready = sem("index_ready")
        index_step = sem("index_step")
        tail_clear = sem("tail_clear")
        least_ready = sem("least_ready")
        least_turned = sem("least_turned")
        ahead_ready = sem("ahead_ready")
        w1_ready = sem("w1_ready")
        be0_w1 = sem("be0_w1")
        hot_ready = sems("hot_ready", 2)
        hot_part_ready = sems("hot_part_ready", 2)
        part_taken = sems("part_taken", 2)
        hot_used = sems("hot_used", 2)
        deg_ready = sem("deg_ready")
        deg_root = sem("deg_root")
        newton_step = sem("newton_step")
        dis_ready = sem("dis_ready")
        begun = sem("begun")
        sp_begun = sem("sp_begun")
        c_in, c_scaled, c_turned, c_evicted, c_mm = (
            sems(n, 2) for n in ("c_in", "c_scaled", "c_turned", "c_evicted", "c_mm"))
        c_tanh, c_step, c_var, c_rstd, c_ab, c_applied, c_column, c_stored = (
            sems(n, 4) for n in ("c_tanh", "c_step", "c_var", "c_rstd", "c_ab", "c_applied", "c_column", "c_stored"))
        d_shifted, d_gained, d_summed, d_skip, d_skip_stored = (
            sems(n, 2) for n in ("d_shifted", "d_gained", "d_summed", "d_skip", "d_skip_stored"))
        d_x, d_step, d_var, d_rstd, d_ab, d_relu = (
            sems(n, 4) for n in ("d_x", "d_step", "d_var", "d_rstd", "d_ab", "d_relu"))
        m_stored = sems("m_stored", 4)
        m_turned, m_evicted, m_mm1, m_hidden, m_mm2, m_out = (
            sems(n, 2) for n in ("m_turned", "m_evicted", "m_mm1", "m_hidden", "m_mm2", "m_out"))
        e_row, e_same, e_rows, e_step, e_mm, e_summed, e_added, e_attr, e_sum, e_msg = (
            sems(n, 2) for n in ("e_row", "e_same", "e_rows", "e_step", "e_mm", "e_summed", "e_added", "e_attr",
                                 "e_sum", "e_msg"))
        e_src, e_got = sems("e_src", 4), sems("e_got", 4)

        def all_done(eng, ring_sems, total, passes, value):
            for j, s in enumerate(ring_sems):
                eng.wait_ge(s, value * passes * len(range(j, total, len(ring_sems))))

        def rounds(eng, one_round):
            eng.wait_ge(ahead_ready, 1)
            flag = eng.value_load(ahead[0:1, 0:1], min_val=0, max_val=1)
            with eng.If(flag > 0):
                for r in range(3):
                    one_round(r, LEAD)
            with eng.Else():
                for r in range(3):
                    one_round(r, GROUPS)

        block = ctx.enter_context(nc.Block())

        @block.sync
        def _(sp):
            sp.wait_ge(tail_clear, 1)
            for tile, v in ((dst_i, dst), (src_i, src)):
                full = (GROUPS - 1) * GROUP
                sp.dma_start(tile[:, 0:PER_P - U].rearrange("p (g u) -> p g u", u=U),
                             v[0:full].rearrange("(g p u) -> p g u", p=P, u=U)).then_inc(edges_in, 16)
                sp.dma_start(tile[0:TAIL_E, PER_P - U:PER_P],
                             v[full:E].rearrange("(p u) -> p u", u=U)).then_inc(edges_in, 16)
            for tile, w, b in ((w0a, w0, b0), (mw2a, mw2, mb2)):
                sp.dma_start(tile[0:D, :], w).then_inc(weights_in, 16)
                sp.dma_start(tile[D:D + 1, :], row(b)).then_inc(weights_in, 16)
            sp.dma_start(w1s[:, :], w1).then_inc(weights_in, 16)
            sp.dma_start(w1a[D + 1:D + 2, :], row(b1)).then_inc(weights_in, 16)
            sp.dma_start(mw1s[:, :], mw1).then_inc(weights_in, 16)
            for tile, v in ((mb1s, mb1), (g0c, g0), (be0c, be0)):
                sp.dma_start(tile[:, :], v.rearrange("(d a) -> d a", a=1)).then_inc(weights_in, 16)
            for tile, v in ((gain1, g1), (shift1, be1)):
                sp.dma_start(tile[:, :], row(v).to_broadcast([P, D])).then_inc(weights_in, 16)
            sp.wait_ge(consts_ready, 1)
            for t, w in ((accum_d, D), (accum_w, WIDE)):
                sp.dma_start(t[SPARE:SPARE + GROUP, :].rearrange("(p u) d -> p (u d)", u=U),
                             zeros[:, 0:U * w]).then_inc(spare_zeroed, 16)

            def load_x0(it):
                j, n = it.of(4)
                sp.wait_ge(c_tanh[j], n)
                parts = block_parts(it)
                sp.dma_start(x_in[j][0:parts, :, :].rearrange("p s d -> p (s d)"),
                             rows(x, it.index, parts)).then_inc(d_x[j], 16)
            run_steps(sp, 4, [blocks(0, load_x0)])

            def one_round(r, lead):
                z = lead + 4

                def load_row(it):
                    j, n = it.of(2, r)
                    sp.wait_ge(e_same[j], n)
                    if r == 0:
                        sp.wait_ge(e_rows[j], n)
                    edges = edge_parts(it) * U
                    sp.dma_start(dst_row[j][:, 0:edges],
                                 row(dst)[:, ds(it.index * GROUP, edges)].to_broadcast([P, edges])
                                 ).then_inc(e_row[j], 16)

                def load_attr(it):
                    j, n = it.of(2)
                    sp.wait_ge(e_sum[j], n)
                    parts = edge_parts(it)
                    sp.dma_start(attr[j][0:parts, :, :].rearrange("p u d -> p (u d)"),
                                 edge_attr[ds(it.index * GROUP, parts * U), :].rearrange("(p u) d -> p (u d)", u=U)
                                 ).then_inc(e_attr[j], 16)

                def group_added(it):
                    g = Item(it.at, it.per, it.c + lead, GROUPS)
                    j, n = g.of(2, r)
                    sp.wait_ge(e_added[j], 16 * U * (n + 1))
                    sp.sem_inc(sp_begun, 1)

                def load_accum(it):
                    j, n = it.of(2, r)
                    if r < 2:
                        sp.wait_ge(c_scaled[j], n)
                    else:
                        last = Item(it.at, 2 * it.per, 2 * it.c - 3, 2 * BLOCKS)
                        if it.at is not None or it.c >= 2:
                            q, m = last.of(2)
                            sp.wait_ge(m_turned[q], m + 1)
                    sp.dma_start(a_in[j][:, 0:S * widths[r]], rows(accums[r], it.index)
                                 ).then_inc(c_in[j], 16)

                def load_early(it):
                    group_added(it)
                    load_accum(it)

                def load_late(it):
                    all_done(sp, e_added, GROUPS, r + 1, 16 * U)
                    load_accum(it)

                def load_x(it):
                    j, n = it.of(4)
                    if r == 1:
                        q, m = Item(it.at, it.per, it.c - 4, BLOCKS).of(2)
                        if it.at is not None or it.c >= 4:
                            sp.wait_ge(d_shifted[q], m + 1)
                        parts = block_parts(it)
                        sp.dma_start(x_in[j][0:parts, :, :].rearrange("p s d -> p (s d)"),
                                     rows(x, it.index, parts)).then_inc(d_x[j], 16)
                    else:
                        if it.at is not None or it.c >= 4:
                            q, m = Item(it.at, 2 * it.per, 2 * it.c - 7, 2 * BLOCKS).of(2)
                            sp.wait_ge(m_out[q], m + 1)
                        sp.dma_start(x_in[j][:, :, :].rearrange("p s d -> p (s d)"),
                                     rows(skip, it.index)).then_inc(d_x[j], 16)

                if r == 2:
                    all_done(sp, d_skip_stored, BLOCKS, 1, 16)
                stages = [groups(-3, load_row)]
                if r == 2:
                    stages.append(groups(-3, load_attr))
                stages += [blocks(z - 1, load_early, 0, GROUPS - lead), blocks(z - 1, load_late, GROUPS - lead)]
                if r == 1:
                    stages.append(blocks(z + 5, load_x))
                if r == 2:
                    stages.append(blocks(z, load_x))
                run_steps(sp, 4, stages)
            rounds(sp, one_round)

        def shift_x(eng):
            def stage(it):
                j, n = it.of(2)
                q, m = it.of(4, 1)
                eng.wait_ge(d_x[q], 16 * (m + 1))
                eng.wait_ge(d_summed[j], n)
                eng.tensor_tensor(shifted[j][:, :, :], x_in[q][:, :, :],
                                  shift1[:, :].unsqueeze(1).to_broadcast([P, S, D]), ALU.add
                                  ).then_inc(d_shifted[j], 1)
            return stage

        def add_skip(eng):
            def stage(it):
                j, n = it.of(2)
                q, m = it.of(4)
                eng.wait_ge(d_relu[q], m + 1)
                eng.wait_ge(d_skip_stored[j], 16 * n)
                eng.tensor_tensor(x_plus_h[j][:, :, :], x1[q][:, :, :], wide(h_out[q], D), ALU.add
                                  ).then_inc(d_skip[j], 1)
            return stage

        @block.gpsimd
        def _(pool):
            pool.memset(zeros[:, :], 0.0)
            pool.memset(neg_half[:, :], -0.5)
            pool.memset(ident[:, :], 0.0).then_inc(fill, 1)
            pool.iota(count_up[:, :], [[1, COLS]], base=0, channel_multiplier=0, allow_small_or_imprecise_dtypes=True)
            pool.iota(place[:, :], [[1, GROUP]], base=0, channel_multiplier=-U, allow_small_or_imprecise_dtypes=True)
            pool.iota(spare_f[:, :], [[P, U]], base=SPARE, channel_multiplier=1, allow_small_or_imprecise_dtypes=True)
            pool.iota(earliest[:, :, :], [[BLOCK, GROUPS], [0, U]], base=-LEAD * BLOCK, channel_multiplier=0,
                      allow_small_or_imprecise_dtypes=True)
            pool.wait_ge(fill, 1)
            pool.affine_select(out=ident[:, :], in_=ident[:, :], compare_op=ALU.not_equal, fill=1.0,
                               base=0, pattern=[[-1, P]], channel_multiplier=1).then_inc(consts_ready, 1)

            def hot_parts(it):
                j, n = it.of(2)
                pool.wait_ge(hot_used[j], n)
                pool.wait_ge(part_taken[j], n + 1)
                pool.sem_inc(begun, 1)
                for u in range(U):
                    last = pool.tensor_scalar(hot_part[j][:, u, :], count_up[:, 0:P], part_slot[j][:, u:u + 1], None,
                                              ALU.is_equal)
                last.then_inc(hot_part_ready[j], 1)
            pool.wait_ge(consts_ready, 1)
            run_steps(pool, 4, [groups(0, hot_parts)])

            def power(var_ready, var_t, rstd_t, rstd_ready, passes=0):
                def stage(it):
                    j, n = it.of(4, passes)
                    pool.wait_ge(var_ready[j], n + 1)
                    pool.tensor_tensor(rstd_t[j][:, :], var_t[j][:, :], neg_half[:, :].to_broadcast([P, S]),
                                       ALU.pow).then_inc(rstd_ready[j], 1)
                return stage

            run_steps(pool, 4, [blocks(0, power(c_var, var, rstd, c_rstd))])
            pool.wait_ge(spare_zeroed, 32)
            all_done(pool, c_stored, BLOCKS, 1, 32)

            def one_round(r, lead):
                z = lead + 4
                if r > 0:
                    all_done(pool, c_stored, BLOCKS, r + 1, 32)

                def scatter(it):
                    j, n = it.of(2, r)
                    pool.wait_ge(e_summed[j], n + 1)
                    pool.wait_ge(e_rows[j], n + 1)
                    pool.wait_ge(e_added[1 - j], 16 * U * (n + j))
                    pool.sem_inc(begun, 1)
                    parts = edge_parts(it)
                    for u in range(U):
                        pool.indirect_dma_start(
                            out=accums[r][:, :],
                            out_offset=bass.IndirectOffsetOnAxis(ap=row_slot[j][0:parts, u:u + 1], axis=0),
                            in_=summed[j][0:parts, u, 0:widths[r]], in_offset=None, compute_op=ALU.add
                        ).then_inc(e_added[j], 16)

                def gather(it):
                    j, n = it.of(4, r)
                    pool.wait_ge(e_src[j], n + 1)
                    pool.sem_inc(begun, 1)
                    parts = edge_parts(it)
                    for u in range(U):
                        pool.indirect_dma_start(
                            out=got[j][0:parts, u, 0:widths[r]], out_offset=None, in_=tables[r][:, :],
                            in_offset=bass.IndirectOffsetOnAxis(ap=src_slot[j][0:parts, u:u + 1], axis=0)
                        ).then_inc(e_got[j], 16)
                stages = [groups(0, scatter), groups(-3, gather)]
                if r < 2:
                    stages.append(blocks(z + 5, power(c_var, var, rstd, c_rstd, r + 1)))
                if r == 1:
                    late = GROUPS - z
                    stages += [blocks(z + 7, shift_x(pool), late), blocks(z + 11, add_skip(pool), late),
                               blocks(z + 9, power(d_var, var_b, rstd_b, d_rstd))]
                run_steps(pool, 4, stages)
            rounds(pool, one_round)

        @block.vector
        def _(dve):
            dve.memset(dst_i[:, PER_P - U:PER_P], PADDED)
            dve.memset(src_i[:, PER_P - U:PER_P], 0).then_inc(tail_clear, 1)
            for j in range(2):
                dve.memset(turned[j][D:D + 2, :], 1.0)
                dve.memset(hidden[j][D:D + 1, :], 1.0).then_inc(ones_ready, 1)
            dve.wait_ge(edges_in, 64)
            dve.tensor_copy(dst_f[:, :], dst_i[:, :])
            dve.tensor_scalar(part_i[:, :], dst_i[:, :], 3, P - 1, ALU.arith_shift_right, ALU.bitwise_and)
            dve.tensor_scalar(high_i[:, :], dst_i[:, :], 10, 3, ALU.arith_shift_right, ALU.logical_shift_left)
            dve.tensor_scalar(low_i[:, :], dst_i[:, :], S - 1, None, ALU.bitwise_and).then_inc(index_step, 1)
            dve.wait_ge(index_step, 1)
            dve.tensor_copy(part_f[:, :], part_i[:, :])
            dve.tensor_tensor(col_f[:, :], high_i[:, :], low_i[:, :], ALU.add).then_inc(index_step, 1)
            dve.wait_ge(consts_ready, 1)
            dve.tensor_tensor(slack[:, :], dst_f[:, :], earliest[:, :, :].rearrange("p g u -> p (g u)"),
                              ALU.subtract).then_inc(least_ready, 1)
            dve.wait_ge(least_ready, 1)
            dve.tensor_reduce(least[:, :], slack[:, :], op=ALU.min, axis=AX.X).then_inc(least_ready, 1)
            dve.tensor_tensor(dst_sp[:, :].rearrange("p (g u) -> p g u", u=U),
                              dst_f[:, :].rearrange("p (g u) -> p g u", u=U),
                              spare_f[:, :].unsqueeze(1).to_broadcast([P, GROUPS, U]), ALU.subtract)
            for u in range(U):
                dve.tensor_scalar(before[:, u, :], place[:, :], float(u), None, ALU.is_lt).then_inc(index_ready, 1)
            dve.wait_ge(least_turned, 1)
            dve.tensor_reduce(least_all[:, :], ps_out[1][0:1, 1, 0:P], op=ALU.min, axis=AX.X).then_inc(least_ready, 1)
            dve.wait_ge(least_ready, 3)
            dve.tensor_scalar(ahead[:, :], least_all[:, :], 0.0, None, ALU.is_ge).then_inc(ahead_ready, 1)
            dve.wait_ge(index_step, 2)

            def one_hot(it):
                j, n = it.of(2)
                dve.wait_ge(hot_used[j], n)
                for u in range(U):
                    last = dve.tensor_scalar(hot_col[j][:, u, :], count_up[:, :], col_f[:, ds(it.index * U + u, 1)],
                                             None, ALU.is_equal)
                last.then_inc(hot_ready[j], 1)
            run_steps(dve, 4, [groups(0, one_hot)])
            dve.wait_ge(weights_in, 16 * 12)
            dve.tensor_scalar(w1a[0:D, :], w1s[:, :], g0c[:, :], None, ALU.mult).then_inc(w1_ready, 1)
            dve.wait_ge(be0_w1, 1)
            dve.tensor_copy(w1a[D:D + 1, :], ps_out[1][0:1, 0, 0:D]).then_inc(w1_ready, 1)
            dve.tensor_scalar(deg[:, :].rearrange("p (h c) -> p h c", h=2), ps_turn[:, :, 0:HALF], 1.0, None,
                              ALU.add).then_inc(deg_ready, 1)
            dve.wait_ge(deg_root, 1)
            dve.reciprocal(dis[:, :], newton[:, :]).then_inc(newton_step, 1)
            dve.wait_ge(newton_step, 1)
            dve.tensor_tensor(newton[:, :], dis[:, :], dis[:, :], ALU.mult).then_inc(newton_step, 1)
            dve.wait_ge(newton_step, 2)
            dve.scalar_tensor_tensor(out=deg[:, :], in0=newton[:, :], scalar=-0.5, in1=deg[:, :],
                                     op0=ALU.mult, op1=ALU.mult).then_inc(newton_step, 1)
            dve.wait_ge(newton_step, 3)
            dve.scalar_tensor_tensor(out=dis[:, :], in0=deg[:, :], scalar=1.5, in1=dis[:, :],
                                     op0=ALU.add, op1=ALU.mult).then_inc(dis_ready, 1)

            def variance(st, m2, md, ms, md2, va, step, src_t, var_ready, passes=0):
                def stage(it):
                    j, n = it.of(4, passes)
                    s = step[j]
                    for i in range(S):
                        last = dve.bn_stats(st[j][:, i, :], src_t[j][:, i, :])
                    last.then_inc(s, 1)
                    dve.wait_ge(s, 3 * n + 1)
                    dve.tensor_tensor(md[j][:, :], st[j][:, :, 1], st[j][:, :, 4], ALU.subtract).then_inc(s, 1)
                    dve.tensor_tensor(m2[j][:, :], st[j][:, :, 1], st[j][:, :, 4], ALU.add)
                    dve.scalar_tensor_tensor(out=ms[j][:, :], in0=st[j][:, :, 2], scalar=EPS * D,
                                             in1=st[j][:, :, 5], op0=ALU.add, op1=ALU.add)
                    dve.wait_ge(s, 3 * n + 2)
                    dve.scalar_tensor_tensor(out=md2[j][:, :], in0=md[j][:, :], scalar=0.25, in1=md[j][:, :],
                                             op0=ALU.mult, op1=ALU.mult).then_inc(s, 1)
                    dve.wait_ge(s, 3 * n + 3)
                    dve.scalar_tensor_tensor(out=va[j][:, :], in0=ms[j][:, :], scalar=1.0 / D, in1=md2[j][:, :],
                                             op0=ALU.mult, op1=ALU.add).then_inc(var_ready[j], 1)
                return stage

            var0 = variance(stats, mean2, mdiff, m2sum, mdiff2, var, c_step, x_in, c_var)

            def stats0(it):
                j, n = it.of(4)
                dve.wait_ge(d_x[j], 16 * (n + 1))
                var0(it)

            def scales0(it):
                j, n = it.of(4)
                dve.wait_ge(c_rstd[j], n + 1)
                dve.tensor_tensor(ln_a[j][:, :], rstd[j][:, :], dis[:, ds(it.index * S, S)], ALU.mult
                                  ).then_inc(c_ab[j], 1)
                dve.wait_ge(c_ab[j], 2 * n + 1)
                dve.scalar_tensor_tensor(out=ln_b[j][:, :], in0=mean2[j][:, :], scalar=-0.5, in1=ln_a[j][:, :],
                                         op0=ALU.mult, op1=ALU.mult).then_inc(c_ab[j], 1)

            def apply0(it):
                j, n = it.of(4)
                dve.wait_ge(c_ab[j], 2 * n + 2)
                dve.wait_ge(c_applied[j], n)
                for i in range(S):
                    last = dve.tensor_scalar(tanhs[j][:, i, :], x_in[j][:, i, :], ln_a[j][:, i:i + 1],
                                             ln_b[j][:, i:i + 1], ALU.mult, ALU.add)
                last.then_inc(c_tanh[j], 1)
            dve.wait_ge(dis_ready, 1)
            dve.wait_ge(index_ready, U)
            run_steps(dve, 4, [blocks(2, scales0), blocks(0, stats0), blocks(2, apply0)])

            def one_round(r, lead):
                z = lead + 4

                def compare(it):
                    j, n = it.of(2, r)
                    dve.wait_ge(e_row[j], 16 * (n + 1))
                    dve.wait_ge(e_mm[j], n)
                    parts = edge_parts(it)
                    for u in range(U):
                        last = dve.tensor_scalar(same[j][0:parts, u, 0:parts * U], dst_row[j][0:parts, 0:parts * U],
                                                 dst_f[0:parts, ds(it.index * U + u, 1)], None, ALU.is_equal)
                    last.then_inc(e_same[j], 1)

                def choose(it):
                    j, n = it.of(2)
                    parts = edge_parts(it)
                    for u in range(U):
                        last = dve.scalar_tensor_tensor(
                            out=junk[0:parts, u, 0:parts * U], in0=dst_row[j][0:parts, 0:parts * U],
                            scalar=dst_f[0:parts, ds(it.index * U + u, 1)], in1=before[0:parts, u, 0:parts * U],
                            op0=ALU.is_equal, op1=ALU.mult, accum_out=earlier[j][0:parts, u:u + 1])
                    last.then_inc(e_step[j], 1)
                    dve.wait_ge(e_step[j], 3 * n + 1)
                    dve.scalar_tensor_tensor(out=chosen[j][:, :], in0=earlier[j][:, :], scalar=0.0,
                                             in1=dst_sp[:, ds(it.index * U, U)], op0=ALU.is_equal, op1=ALU.mult
                                             ).then_inc(e_step[j], 1)
                    dve.wait_ge(e_step[j], 3 * n + 2)
                    dve.tensor_tensor(row_i[:, ds(it.index * U, U)], chosen[j][:, :], spare_f[:, :], ALU.add
                                      ).then_inc(e_step[j], 1)

                def take_rows(it):
                    j, n = it.of(2, r)
                    if r == 0:
                        dve.wait_ge(e_step[j], 3 * n + 3)
                    dve.wait_ge(e_added[j], 16 * U * n)
                    dve.tensor_scalar(row_slot[j][:, :], row_i[:, ds(it.index * U, U)], 0.0, None, ALU.add
                                      ).then_inc(e_rows[j], 1)

                def add_attr(it):
                    j, n = it.of(2)
                    q, m = it.of(4, r)
                    dve.wait_ge(e_got[q], 16 * U * (m + 1))
                    dve.wait_ge(e_attr[j], 16 * (n + 1))
                    dve.wait_ge(e_mm[j], n + 2 * len(range(j, GROUPS, 2)))
                    parts = edge_parts(it)
                    dve.tensor_tensor(message[j][0:parts, :, :], got[q][0:parts, :, 0:D], attr[j][0:parts, :, :],
                                      ALU.add).then_inc(e_sum[j], 1)
                    dve.wait_ge(e_sum[j], n + 1)
                    dve.tensor_scalar(message[j][0:parts, :, :], message[j][0:parts, :, :], 0.0, None, ALU.max
                                      ).then_inc(e_msg[j], 1)
                stages = [groups(-2, compare)]
                if r == 0:
                    stages.append(groups(-2, choose))
                stages.append(groups(-1, take_rows))
                if r == 2:
                    stages.append(groups(-2, add_attr))

                def scale(it):
                    j, n = it.of(2, r)
                    dve.wait_ge(c_in[j], 16 * (n + 1))
                    dve.wait_ge(c_turned[j], n)
                    dve.tensor_tensor(wide(scaled[j], widths[r]), wide(a_in[j], widths[r]),
                                      dis[:, ds(it.index * S, S)].unsqueeze(2).to_broadcast([P, S, widths[r]]),
                                      ALU.mult).then_inc(c_scaled[j], 1)

                var1 = variance(stats, mean2, mdiff, m2sum, mdiff2, var, c_step, tanhs, c_var, r + 1)

                def stats1(it):
                    j, n = it.of(4, r + 1)
                    dve.wait_ge(c_tanh[j], n + 1)
                    var1(it)

                def scales1(it):
                    j, n = it.of(4, r + 1)
                    dve.wait_ge(c_rstd[j], n + 1)
                    dve.wait_ge(c_applied[j], n)
                    if r == 1:
                        dve.tensor_scalar(ln_a[j][:, :], rstd[j][:, :], 1.0, None, ALU.mult).then_inc(c_ab[j], 1)
                    else:
                        dve.tensor_tensor(ln_a[j][:, :], rstd[j][:, :], dis[:, ds(it.index * S, S)], ALU.mult
                                          ).then_inc(c_ab[j], 1)
                    dve.wait_ge(c_ab[j], 2 * n + 1)
                    dve.scalar_tensor_tensor(out=ln_b[j][:, :], in0=mean2[j][:, :], scalar=-0.5, in1=ln_a[j][:, :],
                                             op0=ALU.mult, op1=ALU.mult).then_inc(c_ab[j], 1)

                def column(it):
                    j, n = it.of(4)
                    _, m = it.of(4, r + 1)
                    dve.wait_ge(c_stored[j], 32 * m)
                    dve.tensor_scalar(wide(h_out[j], WIDE)[:, :, D], dis[:, ds(it.index * S, S)], 1.0, None,
                                      ALU.mult).then_inc(c_column[j], 1)

                def gain(it):
                    j, n = it.of(2)
                    q, m = it.of(4, r + 1)
                    dve.wait_ge(c_applied[q], m + 1)
                    dve.wait_ge(d_summed[j], n)
                    dve.tensor_tensor(gained[j][:, :, :], normed[j][:, :, :],
                                      gain1[:, :].unsqueeze(1).to_broadcast([P, S, D]), ALU.mult
                                      ).then_inc(d_gained[j], 1)

                var2 = variance(stats_b, mean2_b, mdiff_b, m2sum_b, mdiff2_b, var_b, d_step, x1, d_var)

                def residual(it):
                    j, n = it.of(2)
                    q, m = it.of(4)
                    dve.wait_ge(d_gained[j], n + 1)
                    dve.wait_ge(d_shifted[j], n + 1)
                    k, o = Item(it.at, it.per, it.c - 4, BLOCKS).of(2)
                    if it.at is not None or it.c >= 4:
                        dve.wait_ge(d_skip[k], o + 1)
                    dve.tensor_tensor(x1[q][:, :, :], gained[j][:, :, :], shifted[j][:, :, :], ALU.add
                                      ).then_inc(d_summed[j], 1)
                    dve.wait_ge(d_summed[j], n + 1)
                    var2(it)

                def scales2(it):
                    j, n = it.of(4)
                    dve.wait_ge(d_rstd[j], n + 1)
                    dve.wait_ge(d_relu[j], n)
                    dve.scalar_tensor_tensor(out=ln_b_b[j][:, :], in0=mean2_b[j][:, :], scalar=-0.5,
                                             in1=rstd_b[j][:, :], op0=ALU.mult, op1=ALU.mult).then_inc(d_ab[j], 1)

                def finish(it):
                    h, n = it.of(2)
                    b = Item(it.at, it.per // 2, it.c // 2, BLOCKS)
                    j, m = b.of(4)
                    dve.wait_ge(m_mm2[h], n + 1)
                    if h == 0:
                        dve.wait_ge(d_x[j], 16 * (b.of(4, 2)[1] + 1))
                        dve.wait_ge(m_stored[j], 16 * m)
                    dve.scalar_tensor_tensor(
                        out=h_out[j][:, h * HS:(h + 1) * HS], in0=ps_out[1][:, h, 0:HS], scalar=0.0,
                        in1=x_in[j][:, :, :].rearrange("p s d -> p (s d)")[:, h * HS:(h + 1) * HS],
                        op0=ALU.max, op1=ALU.add).then_inc(m_out[h], 1)

                if r == 2:
                    stages.append(halves(2 * z + 5, finish))
                else:
                    stages += [blocks(z, scale), blocks(z + 6, scales1)]
                    if r == 1:
                        early = GROUPS - z
                        stages += [blocks(z + 8, gain), blocks(z + 7, shift_x(dve), 0, early),
                                   blocks(z + 10, scales2), blocks(z + 11, add_skip(dve), 0, early)]
                    else:
                        stages.append(blocks(z + 6, column))
                    stages.append(blocks(z + 4, stats1))
                    if r == 1:
                        stages.append(blocks(z + 8, residual))
                run_steps(dve, 4, stages)
            rounds(dve, one_round)

        @block.scalar
        def _(act):
            act.wait_ge(index_step, 2)

            def take_parts(it):
                j, n = it.of(2)
                act.wait_ge(hot_part_ready[j], n)
                act.copy(part_slot[j][:, :], part_f[:, ds(it.index * U, U)]).then_inc(part_taken[j], 1)
            run_steps(act, 4, [groups(0, take_parts)])
            act.wait_ge(deg_ready, 1)
            act.activation(newton[:, :], deg[:, :], ACT.Sqrt).then_inc(deg_root, 1)

            def relu0(it):
                j, n = it.of(4)
                act.wait_ge(c_tanh[j], n + 1)
                act.wait_ge(c_stored[j], 32 * n)
                act.activation(h_out[j][:, 0:S * D], tanhs[j][:, :, :].rearrange("p s d -> p (s d)"), ACT.Relu
                               ).then_inc(c_applied[j], 1)

            def store0(it):
                j, n = it.of(4)
                act.wait_ge(c_applied[j], n + 1)
                for t in (table_d, accum_d):
                    act.dma_start(rows(t, it.index), h_out[j][:, 0:S * D]).then_inc(c_stored[j], 16)
            run_steps(act, 4, [blocks(3, store0), blocks(2, relu0)])

            def one_round(r, lead):
                z = lead + 4

                def take_src(it):
                    j, n = it.of(4, r)
                    act.wait_ge(e_got[j], 16 * U * n)
                    if it.at is not None or it.c >= 4:
                        q, m = Item(it.at, it.per, it.c - 4, GROUPS).of(2, r)
                        act.wait_ge(e_mm[q], m + 1)
                    act.copy(src_slot[j][:, :], src_i[:, ds(it.index * U, U)]).then_inc(e_src[j], 1)

                def evict_sums(it):
                    j, n = it.of(2, r)
                    act.wait_ge(e_mm[j], n + 1)
                    act.wait_ge(e_added[j], 16 * U * n)
                    parts = edge_parts(it)
                    act.copy(summed[j][0:parts, :, 0:widths[r]],
                             ps_sum[0:parts, j, 0:U * widths[r]].rearrange("p (u d) -> p u d", u=U)
                             ).then_inc(e_summed[j], 1)
                stages = [groups(-1, evict_sums), groups(-4, take_src)]

                def evict(it):
                    j, n = it.of(2, r)
                    act.wait_ge(c_turned[j], n + 1)
                    act.wait_ge(c_mm[j], n)
                    w = widths[r]
                    act.copy(turned[j][0:w, :].rearrange("p (h c) -> p h c", h=2), ps_turn[0:w, :, :]
                             ).then_inc(c_evicted[j], 1)

                def tanh(it):
                    j, n = it.of(2, r)
                    q, m = it.of(4, r + 1)
                    act.wait_ge(c_mm[j], n + 1)
                    act.wait_ge(c_applied[q], m)
                    act.activation(tanhs[q][:, :, :].rearrange("p (h s) d -> p h (s d)", h=2),
                                   ps_out[j][:, :, 0:HS], ACT.Tanh).then_inc(c_tanh[q], 1)

                def apply(it):
                    q, m = it.of(4, r + 1)
                    act.wait_ge(c_ab[q], 2 * m + 2)
                    if r == 1:
                        j, n = it.of(2)
                        act.wait_ge(d_gained[j], n)
                        to = normed[j][:, :, :]
                    else:
                        act.wait_ge(c_stored[q], 32 * m)
                        to = wide(h_out[q], WIDE)
                    for i in range(S):
                        last = act.activation(to[:, i, 0:D], tanhs[q][:, i, :], ACT.Identity,
                                              bias=ln_b[q][:, i:i + 1], scale=ln_a[q][:, i:i + 1])
                    last.then_inc(c_applied[q], 1)

                def apply2(it):
                    q, m = it.of(4)
                    _, m_both = it.of(4, r + 1)
                    act.wait_ge(d_ab[q], m + 1)
                    act.wait_ge(c_stored[q], 32 * m_both)
                    if it.at is not None or it.c >= 4:
                        k, o = Item(it.at, it.per, it.c - 4, BLOCKS).of(2)
                        act.wait_ge(d_skip[k], o + 1)
                    for i in range(S):
                        last = act.activation(wide(h_out[q], D)[:, i, :], x1[q][:, i, :], ACT.Relu,
                                              bias=ln_b_b[q][:, i:i + 1], scale=rstd_b[q][:, i:i + 1])
                    last.then_inc(d_relu[q], 1)

                def store(it):
                    q, m = it.of(4)
                    if r == 1:
                        act.wait_ge(d_relu[q], m + 1)
                    else:
                        act.wait_ge(c_applied[q], it.of(4, r + 1)[1] + 1)
                        act.wait_ge(c_column[q], m + 1)
                    for t in (tables[r + 1], accums[r + 1]):
                        act.dma_start(rows(t, it.index), h_out[q][:, 0:S * widths[r + 1]]).then_inc(c_stored[q], 16)

                def store_skip(it):
                    j, n = it.of(2)
                    act.wait_ge(d_skip[j], n + 1)
                    act.dma_start(rows(skip, it.index), x_plus_h[j][:, :, :].rearrange("p s d -> p (s d)")
                                  ).then_inc(d_skip_stored[j], 16)

                def evict_last(it):
                    j, h, n = half(it)
                    act.wait_ge(m_turned[h], n + 1)
                    if four_back(it):
                        act.wait_ge(m_mm1[h], n - 1)
                    act.copy(turned[j][0:D, h * HB:(h + 1) * HB], ps_turn[0:D, h, :]).then_inc(m_evicted[h], 1)

                def hide(it):
                    j, h, n = half(it)
                    act.wait_ge(m_mm1[h], n + 1)
                    if four_back(it):
                        act.wait_ge(m_mm2[h], n - 1)
                    act.activation(hidden[j][0:D, h * HB:(h + 1) * HB], ps_out[0][0:D, h, :],
                                   ACT.Relu, bias=mb1s[:, :]).then_inc(m_hidden[h], 1)

                def store_out(it):
                    k, o = Item(it.at, 2 * it.per, 2 * it.c + 1, 2 * BLOCKS).of(2)
                    j, n = it.of(4)
                    act.wait_ge(m_out[k], o + 1)
                    parts = block_parts(it)
                    act.dma_start(rows(out, it.index, parts), h_out[j][0:parts, 0:S * D]).then_inc(m_stored[j], 16)

                if r == 0:
                    stages += [blocks(z + 8, store), blocks(z + 1, evict), blocks(z + 7, apply), blocks(z + 3, tanh)]
                elif r == 1:
                    stages += [blocks(z + 11, store), blocks(z + 12, store_skip), blocks(z + 1, evict),
                               blocks(z + 7, apply), blocks(z + 3, tanh), blocks(z + 10, apply2)]
                else:
                    stages += [blocks(z + 4, store_out), halves(2 * z + 1, evict_last), halves(2 * z + 3, hide)]
                run_steps(act, 4, stages)
                if r == 2:
                    all_done(act, m_stored, BLOCKS, 1, 16)
            rounds(act, one_round)

        @block.tensor
        def _(pe):
            pe.wait_ge(least_ready, 2)
            pe.wait_ge(consts_ready, 1)
            pe.transpose(ps_out[1][0:1, 1, 0:P], least[:, :], ident[:, :]).then_inc(least_turned, 1)

            def count(it):
                j, n = it.of(2)
                pe.wait_ge(hot_ready[j], n + 1)
                pe.wait_ge(hot_part_ready[j], n + 1)
                first = it.at is None and it.c == 0
                parts = edge_parts(it)
                for u in range(U):
                    for h in range(2):
                        last = pe.matmul(ps_turn[:, h, 0:HALF], hot_part[j][0:parts, u, :],
                                         hot_col[j][0:parts, u, h * HALF:(h + 1) * HALF],
                                         start=first and u == 0, stop=it.last() and u == U - 1)
                last.then_inc(hot_used[j], 1)
            run_steps(pe, 4, [groups(0, count)])
            pe.wait_ge(weights_in, 16 * 12)
            pe.matmul(ps_out[1][0:1, 0, 0:D], be0c[:, :], w1s[:, :], start=True, stop=True).then_inc(be0_w1, 1)
            pe.wait_ge(w1_ready, 2)
            pe.wait_ge(ones_ready, 2)

            def one_round(r, lead):
                z = lead + 4

                def sums(it):
                    j, n = it.of(2, r)
                    q, m = it.of(4, r)
                    pe.wait_ge(e_same[j], n + 1)
                    if r == 2:
                        pe.wait_ge(e_msg[j], it.of(2)[1] + 1)
                        rhs = message[j]
                    else:
                        pe.wait_ge(e_got[q], 16 * U * (m + 1))
                        rhs = got[q]
                    pe.wait_ge(e_summed[j], n)
                    parts, w = edge_parts(it), widths[r]
                    for i in range(U):
                        for u in range(U):
                            last = pe.matmul(
                                ps_sum[0:parts, j, i * w:(i + 1) * w],
                                same[j][0:parts, u, 0:parts * U].rearrange("p (q i) -> p i q", i=U)[:, i, :],
                                rhs[0:parts, u, 0:w], start=u == 0, stop=u == U - 1)
                    last.then_inc(e_mm[j], 1)

                def turn(it):
                    j, n = it.of(2, r)
                    w = widths[r]
                    pe.wait_ge(c_scaled[j], n + 1)
                    pe.wait_ge(c_evicted[1 - j], n + j)
                    for i in range(S):
                        last = pe.transpose(ps_turn[0:w, i // 4, (i % 4) * P:(i % 4 + 1) * P],
                                            wide(scaled[j], w)[:, i, :], ident[:, :])
                    last.then_inc(c_turned[j], 1)

                def project(it):
                    j, n = it.of(2, r)
                    w = widths[r]
                    pe.wait_ge(c_evicted[j], n + 1)
                    k, o = Item(it.at, it.per, it.c - 2, BLOCKS).of(4, r + 1)
                    if it.at is not None or it.c >= 2:
                        pe.wait_ge(c_tanh[k], o + 1)
                    for i in range(S):
                        last = pe.matmul(ps_out[j][:, i // 4, (i % 4) * D:(i % 4 + 1) * D],
                                         turned[j][0:w + 1, i * P:(i + 1) * P], (w0a, w1a)[r][:, :],
                                         start=True, stop=True)
                    last.then_inc(c_mm[j], 1)

                def turn_last(it):
                    j, h, n = half(it)
                    _, m = Item(it.at, it.per // 2, it.c // 2, BLOCKS).of(2, r)
                    pe.wait_ge(c_in[j], 16 * (m + 1))
                    pe.wait_ge(m_evicted[h], n)
                    for i in range(S // 2):
                        last = pe.transpose(ps_turn[0:D, h, i * P:(i + 1) * P],
                                            wide(a_in[j], D)[:, h * S // 2 + i, :], ident[:, :])
                    last.then_inc(m_turned[h], 1)

                def hide_mm(it):
                    j, h, n = half(it)
                    pe.wait_ge(m_evicted[h], n + 1)
                    pe.wait_ge(m_hidden[h], n)
                    pe.matmul(ps_out[0][0:D, h, :], mw1s[:, :], turned[j][0:D, h * HB:(h + 1) * HB],
                              start=True, stop=True).then_inc(m_mm1[h], 1)

                def project_last(it):
                    j, h, n = half(it)
                    pe.wait_ge(m_hidden[h], n + 1)
                    pe.wait_ge(m_out[h], n)
                    for i in range(S // 2):
                        c = h * HB + i * P
                        last = pe.matmul(ps_out[1][:, h, i * D:(i + 1) * D], hidden[j][:, c:c + P], mw2a[:, :],
                                         start=True, stop=True)
                    last.then_inc(m_mm2[h], 1)

                stages = [groups(-1, sums)]
                if r < 2:
                    stages += [blocks(z + 1, turn), blocks(z + 2, project)]
                else:
                    stages += [halves(2 * z, turn_last), halves(2 * z + 2, hide_mm), halves(2 * z + 4, project_last)]
                run_steps(pe, 4, stages)
            rounds(pe, one_round)


_INS = ['x', 'src', 'dst', 'edge_attr_96', 'L0_gnn_W0', 'L0_gnn_b0', 'L0_gnn_g0', 'L0_gnn_be0', 'L0_gnn_W1',
        'L0_gnn_b1', 'L0_gnn_g1', 'L0_gnn_be1', 'L1_gnn_W1', 'L1_gnn_b1', 'L1_gnn_W2', 'L1_gnn_b2']


def kernel(**inputs):
    import numpy as np
    import concourse.bacc as bacc
    from concourse.bass_utils import run_bass_kernel_spmd

    nc = bacc.Bacc("TRN2", target_bir_lowering=False, num_devices=1)
    arrays, args = {}, []
    for name in _INS:
        a = np.ascontiguousarray(inputs[name])
        arrays[f"in_{name}"] = a
        args.append(nc.dram_tensor(f"in_{name}", a.shape, mybir.dt.from_np(a.dtype), kind="ExternalInput").ap())
    x = inputs["x"]
    args.append(nc.dram_tensor("out_0", x.shape, mybir.dt.float32, kind="ExternalOutput").ap())
    gnn_kernel(nc, *args)
    return run_bass_kernel_spmd(nc, [arrays], core_ids=[0]).results[0]["out_0"]
```

```python
from contextlib import ExitStack

import concourse.bass as bass
from concourse import mybir


class Item:

    def __init__(self, at, per, c, total):
        self.at, self.per, self.c, self.total = at, per, c, total
        self.index = c if at is None else at * per + c

    def of(self, ring, passes=0):
        slot = self.c % ring
        n = self.c // ring + passes * len(range(slot, self.total, ring))
        if self.at is not None:
            n = self.at * (self.per // ring) + n if self.per != ring else self.at + n
        return slot, n

    def last(self):
        return self.at is None and self.c == self.total - 1


def run_steps(eng, per_turn, stages):
    def events(turn):
        found = []
        for order, (lag, stage, items, total, lo, hi) in enumerate(stages):
            for j in range(items):
                i = turn * items + j - lag
                if lo <= i < hi:
                    found.append((j / items, order, i, i < 4 or i == total - 1))
        return sorted(found)

    def run(turn, at):
        for _, order, i, _ in events(turn):
            lag, stage, items, total, lo, hi = stages[order]
            if at is None:
                stage(Item(None, items, i, total))
            else:
                stage(Item(at, items, i - turn * items, total))

    first = min((s[0] + s[4]) // s[2] for s in stages)
    end = max(-(-(s[0] + s[5]) // s[2]) for s in stages)
    kinds = [([(p, o) for p, o, _, _ in events(t)], any(e[3] for e in events(t))) for t in range(first, end)]
    t = first
    while t < end:
        stretch = 1
        while t + stretch < end and not kinds[t - first][1] and kinds[t + stretch - first] == kinds[t - first]:
            stretch += 1
        if stretch >= 3 and t > 0:
            with eng.Fori(t, t + stretch) as at:
                run(t, at)
        else:
            for s in range(t, t + stretch):
                run(s, None)
        t += stretch


def gnn_kernel(nc, x, src, dst, edge_attr, w0, b0, g0, be0, w1, b1, g1, be1, mw1, mb1, mw2, mb2, out):
    fp32, fp16, bf16, i32 = mybir.dt.float32, mybir.dt.float16, mybir.dt.bfloat16, mybir.dt.int32
    ALU = mybir.AluOpType
    ACT = mybir.ActivationFunctionType
    AX = mybir.AxisListType
    ds = bass.ds

    N, D = x.shape
    E = src.shape[0]
    P, S = 128, 8
    BLOCK = P * S
    BLOCKS = -(-N // BLOCK)
    PADDED = BLOCKS * BLOCK
    TAIL_P = (N - (BLOCKS - 1) * BLOCK) // S
    U = 4
    GROUP = P * U
    GROUPS = -(-E // GROUP)
    PER_P = GROUPS * U
    TAIL_E = (E - (GROUPS - 1) * GROUP) // U
    WIDE = D + 1
    SPARE = PADDED
    COLS = BLOCKS * S
    HALF = COLS // 2
    EPS = 1e-5
    HS = S // 2 * D
    HB = BLOCK // 2
    ROOT_GUESS = 0x5F3759DF
    ROOT_OPS = 10
    LEAD = 26
    HOT_V, ROWS_V = 1, 3
    FASTER = 76
    FIRST_FAST = FASTER - LEAD - 3
    assert TAIL_P * S == N - (BLOCKS - 1) * BLOCK and TAIL_E * U == E - (GROUPS - 1) * GROUP
    assert HALF <= 512 and U * WIDE <= 512 and LEAD % 2 == 0 and LEAD < FASTER < GROUPS and FASTER % 4 == 0

    table_d, table_w = (nc.dram_tensor(n, (PADDED, w), fp32, kind="Internal").ap()
                        for n, w in (("table_d", D), ("table_w", WIDE)))
    accum_d, accum_w = (nc.dram_tensor(n, (PADDED + GROUP, w), fp32, kind="Internal").ap()
                        for n, w in (("accum_d", D), ("accum_w", WIDE)))
    tables, accums, widths = (table_d, table_w, table_d), (accum_d, accum_w, accum_d), (D, WIDE, D)
    skip = nc.dram_tensor("skip", (PADDED, D), fp32, kind="Internal").ap()

    def rows(t, blk, parts=P):
        return t[ds(blk * BLOCK, parts * S), :].rearrange("(p s) d -> p (s d)", s=S)

    def wide(t, w):
        return t[:, 0:S * w].rearrange("p (s d) -> p s d", s=S)

    def row(v):
        return v.rearrange("(a d) -> a d", a=1)

    def block_parts(it):
        return TAIL_P if it.last() else P

    def edge_parts(it):
        return TAIL_E if it.last() else P

    def groups(lag, stage):
        return (lag, stage, 4, GROUPS, 0, GROUPS)

    def behind(r, lead):
        z = lead + 4
        fast = lead == LEAD and r == 2

        def at_step(d, k):
            return max(0, k - z - d + (max(0, k - FASTER) if fast else 0))

        def make(d, stage, lo, hi, per_block, split):
            items, total, lag = 4 * per_block, per_block * BLOCKS, per_block * z + d
            if not fast:
                return [(lag, stage, items, total, lo, hi)]
            return [(lag, stage, items, total, lo, min(split, hi)),
                    (2 * per_block * FASTER - split, stage, 2 * items, total, max(split, lo), hi)]

        def blocks(d, stage, lo=0, hi=BLOCKS):
            return make(d, stage, lo, hi, 1, FASTER - z - d)

        def halves(d, stage):
            return make(d, stage, 0, 2 * BLOCKS, 2, 2 * (FASTER - z) - d)
        return blocks, halves, at_step

    def first_blocks(lag, stage):
        return (lag, stage, 8, BLOCKS, 0, BLOCKS)

    def half(it):
        h, n = it.of(2)
        return it.c // 2 % 2, h, n

    def four_back(it):
        return it.at is not None or it.c >= 4

    ctx = ExitStack()
    with ctx:
        def sb(name, shape, dt=fp32):
            return ctx.enter_context(nc.sbuf_tensor(name, shape, dt))

        def sbs(name, n, shape, dt=fp32):
            return [sb(f"{name}{i}_", shape, dt) for i in range(n)]

        def sem(name):
            return ctx.enter_context(nc.semaphore(name))

        def sems(name, n):
            return [sem(f"{name}{i}") for i in range(n)]

        ident = sb("ident", [P, P])
        neg_half = sb("neg_half", [P, 1])
        w0a, mw2a = (sb(n, [D + 1, D]) for n in ("w0a", "mw2a"))
        w1a = sb("w1a", [D + 2, D])
        w1s = sb("w1s", [D, D])
        g0c, be0c = sb("g0c", [D, 1]), sb("be0c", [D, 1])
        mw1s = sb("mw1s", [D, D])
        mb1s = sb("mb1s", [D, 1])
        gain1, shift1 = sb("gain1", [P, D]), sb("shift1", [P, D])
        dis = sb("dis", [P, COLS])
        deg = sb("deg", [P, COLS])
        newton = sb("newton", [P, COLS])
        src_i = sb("src_i", [P, PER_P], i32)
        dst_i = sb("dst_i", [P, PER_P], i32)
        dst_f = sb("dst_f", [P, PER_P])
        dst_sp = sb("dst_sp", [P, PER_P])
        row_i = sb("row_i", [P, PER_P], i32)
        part_i = sb("part_i", [P, PER_P], i32)
        high_i = sb("high_i", [P, PER_P], i32)
        low_i = sb("low_i", [P, PER_P], i32)
        part_f = sb("part_f", [P, PER_P])
        col_f = sb("col_f", [P, PER_P])
        earliest = sb("earliest", [P, GROUPS, U])
        slack = sb("slack", [P, PER_P])
        rise = sb("rise", [P, GROUPS, U])
        last_dst = sb("last_dst", [P, GROUPS])
        left_dst = sb("left_dst", [P, GROUPS])
        first_sp = sb("first_sp", [P, PER_P])
        least = sb("least", [P, 1])
        least_all = sb("least_all", [1, 1])
        ahead = sb("ahead", [1, 1], i32)
        count_up = sb("count_up", [P, COLS], fp16)
        part_slot = sbs("part_slot", 2, [P, U])
        hot_part = sbs("hot_part", 2, [P, U, P], bf16)
        hot_col = sbs("hot_col", 2, [P, U, COLS], bf16)
        spare_f = sb("spare_f", [P, U])
        place = sb("place", [P, GROUP])
        before = sb("before", [P, U, GROUP], bf16)
        zeros = sb("zeros", [P, U * WIDE])
        src_slot = sbs("src_slot", 4, [P, U], i32)
        row_slot = sbs("row_slot", 2, [P, U], i32)
        dst_row = sbs("dst_row", 2, [P, GROUP], i32)
        same = sbs("same", 2, [P, U, GROUP])
        junk = sb("junk", [P, U, GROUP], bf16)
        earlier = sbs("earlier", 2, [P, U])
        chosen = sbs("chosen", 2, [P, U])
        got = sbs("got", 4, [P, U, WIDE])
        attr = sbs("attr", 2, [P, U, D])
        message = sbs("message", 2, [P, U, D])
        summed = sbs("summed", 2, [P, U, WIDE])
        x_in = sbs("x_in", 4, [P, S, D])
        a_in = sbs("a_in", 2, [P, S * WIDE])
        scaled = sbs("scaled", 2, [P, S * WIDE])
        turned = sbs("turned", 2, [D + 2, BLOCK])
        hidden = sbs("hidden", 2, [D + 1, BLOCK])
        tanhs = sbs("tanhs", 4, [P, S, D])
        normed = sbs("normed", 2, [P, S, D])
        gained = sbs("gained", 2, [P, S, D])
        shifted = sbs("shifted", 2, [P, S, D])
        x1 = sbs("x1", 4, [P, S, D])
        x_ring = x_in + x1
        h_out = sbs("h_out", 4, [P, S * WIDE])
        x_plus_h = sbs("x_plus_h", 2, [P, S, D])
        stats = sbs("stats", 4, [P, S, 6])
        mean2, mdiff, m2sum, mdiff2, var, rstd, ln_a, ln_b = (
            sbs(n, 4, [P, S]) for n in ("mean2", "mdiff", "m2sum", "mdiff2", "var", "rstd", "ln_a", "ln_b"))
        stats_b = sbs("stats_b", 4, [P, S, 6])
        mean2_b, mdiff_b, m2sum_b, mdiff2_b, var_b, rstd_b, ln_b_b = (
            sbs(n + "_b", 4, [P, S]) for n in ("mean2", "mdiff", "m2sum", "mdiff2", "var", "rstd", "ln_b"))

        root_a, root_b = sbs("root_a", 4, [P, S]), sbs("root_b", 4, [P, S])
        about_a, about_b = sbs("about_a", 4, [P, 3, S]), sbs("about_b", 4, [P, 3, S])
        guess = sb("guess", [P, S], i32)
        power_i = sbs("power_i", 3, [P, S], i32)
        neg_var, square, gap = (sb(n, [P, S]) for n in ("neg_var", "square", "gap"))

        ps = [ctx.enter_context(nc.psum_tensor(f"ps{i}", [P, 2, 512], fp32)) for i in range(4)]
        ps_turn, ps_sum, ps_out = ps[0], ps[1], (ps[2], ps[3])

        edges_in = sem("edges_in")
        weights_in = sem("weights_in")
        spare_zeroed = sem("spare_zeroed")
        consts_ready = sem("consts_ready")
        fill = sem("fill")
        ones_ready = sem("ones_ready")
        index_ready = sem("index_ready")
        index_step = sem("index_step")
        tail_clear = sem("tail_clear")
        last_ready = sem("last_ready")
        left_in = sem("left_in")
        least_ready = sem("least_ready")
        least_turned = sem("least_turned")
        ahead_ready = sem("ahead_ready")
        w1_ready = sem("w1_ready")
        be0_w1 = sem("be0_w1")
        root_step = sem("root_step")
        hot_ready = sems("hot_ready", 2)
        hot_part_ready = sems("hot_part_ready", 2)
        part_taken = sems("part_taken", 2)
        hot_used = sems("hot_used", 2)
        deg_ready = sem("deg_ready")
        deg_root = sem("deg_root")
        newton_step = sem("newton_step")
        dis_ready = sem("dis_ready")
        begun = sem("begun")
        sp_begun = sem("sp_begun")
        c_in, c_scaled, c_turned, c_evicted, c_mm = (
            sems(n, 2) for n in ("c_in", "c_scaled", "c_turned", "c_evicted", "c_mm"))
        c_step, d_step = sem("c_step"), sem("d_step")
        d_ab = sem("d_ab")
        root_a_ready, root_b_ready = sem("root_a_ready"), sem("root_b_ready")
        refine_a, refine_b = sem("refine_a"), sem("refine_b")
        c_tanh, c_var, c_rstd, c_ab, c_applied, c_column, c_stored = (
            sems(n, 4) for n in ("c_tanh", "c_var", "c_rstd", "c_ab", "c_applied", "c_column", "c_stored"))
        p0_x = sems("p0_x", 8)
        d_shifted, d_gained, d_summed, d_skip, d_skip_stored = (
            sems(n, 2) for n in ("d_shifted", "d_gained", "d_summed", "d_skip", "d_skip_stored"))
        d_x, d_var, d_rstd, d_relu = (sems(n, 4) for n in ("d_x", "d_var", "d_rstd", "d_relu"))
        m_stored = sems("m_stored", 4)
        m_turned, m_evicted, m_mm1, m_hidden, m_mm2, m_out = (
            sems(n, 2) for n in ("m_turned", "m_evicted", "m_mm1", "m_hidden", "m_mm2", "m_out"))
        e_row, e_same, e_rows, e_step, e_mm, e_summed, e_added, e_attr, e_sum, e_msg = (
            sems(n, 2) for n in ("e_row", "e_same", "e_rows", "e_step", "e_mm", "e_summed", "e_added", "e_attr",
                                 "e_sum", "e_msg"))
        e_src, e_got = sems("e_src", 4), sems("e_got", 4)

        def all_done(eng, ring_sems, total, passes, value):
            for j, s in enumerate(ring_sems):
                eng.wait_ge(s, value * passes * len(range(j, total, len(ring_sems))))

        def rounds(eng, one_round):
            eng.wait_ge(ahead_ready, 1)
            flag = eng.value_load(ahead[0:1, 0:1], min_val=0, max_val=1)
            with eng.If(flag > 0):
                for r in range(3):
                    one_round(r, LEAD)
            with eng.Else():
                for r in range(3):
                    one_round(r, GROUPS)

        block = ctx.enter_context(nc.Block())

        @block.sync
        def _(sp):
            sp.wait_ge(tail_clear, 1)
            for tile, v in ((dst_i, dst), (src_i, src)):
                full = (GROUPS - 1) * GROUP
                sp.dma_start(tile[:, 0:PER_P - U].rearrange("p (g u) -> p g u", u=U),
                             v[0:full].rearrange("(g p u) -> p g u", p=P, u=U)).then_inc(edges_in, 16)
                sp.dma_start(tile[0:TAIL_E, PER_P - U:PER_P],
                             v[full:E].rearrange("(p u) -> p u", u=U)).then_inc(edges_in, 16)
            sp.wait_ge(last_ready, 1)
            sp.dma_start(left_dst[1:P, :], last_dst[0:P - 1, :]).then_inc(left_in, 16)
            for tile, w, b in ((w0a, w0, b0), (mw2a, mw2, mb2)):
                sp.dma_start(tile[0:D, :], w).then_inc(weights_in, 16)
                sp.dma_start(tile[D:D + 1, :], row(b)).then_inc(weights_in, 16)
            sp.dma_start(w1s[:, :], w1).then_inc(weights_in, 16)
            sp.dma_start(w1a[D + 1:D + 2, :], row(b1)).then_inc(weights_in, 16)
            sp.dma_start(mw1s[:, :], mw1).then_inc(weights_in, 16)
            for tile, v in ((mb1s, mb1), (g0c, g0), (be0c, be0)):
                sp.dma_start(tile[:, :], v.rearrange("(d a) -> d a", a=1)).then_inc(weights_in, 16)
            for tile, v in ((gain1, g1), (shift1, be1)):
                sp.dma_start(tile[:, :], row(v).to_broadcast([P, D])).then_inc(weights_in, 16)
            sp.wait_ge(consts_ready, 1)
            for t, w in ((accum_d, D), (accum_w, WIDE)):
                sp.dma_start(t[SPARE:SPARE + GROUP, :].rearrange("(p u) d -> p (u d)", u=U),
                             zeros[:, 0:U * w]).then_inc(spare_zeroed, 16)

            def load_x0(it):
                j, n = it.of(4)
                if it.at is not None or it.c >= 8:
                    sp.wait_ge(c_applied[j], n - 1)
                parts = block_parts(it)
                k = it.of(8)[0]
                sp.dma_start(x_ring[k][0:parts, :, :].rearrange("p s d -> p (s d)"),
                             rows(x, it.index, parts)).then_inc(p0_x[k], 16)

            def store0(it):
                j, n = it.of(4)
                sp.wait_ge(c_applied[j], n + 1)
                sp.sem_inc(sp_begun, 1)
                for t in (table_d, accum_d):
                    sp.dma_start(rows(t, it.index), h_out[j][:, 0:S * D]).then_inc(c_stored[j], 16)
            run_steps(sp, 8, [first_blocks(-4, load_x0), first_blocks(3, store0)])

            def one_round(r, lead):
                blocks, halves, at_step = behind(r, lead)

                def load_row(it):
                    j, n = it.of(2, r)
                    sp.wait_ge(e_same[j], n)
                    if r == 0 and lead != LEAD:
                        sp.wait_ge(e_rows[j], n)
                    edges = edge_parts(it) * U
                    sp.dma_start(dst_row[j][:, 0:edges],
                                 row(dst)[:, ds(it.index * GROUP, edges)].to_broadcast([P, edges])
                                 ).then_inc(e_row[j], 16)

                def load_attr(it):
                    j, n = it.of(2)
                    sp.wait_ge(e_sum[j], n)
                    parts = edge_parts(it)
                    sp.dma_start(attr[j][0:parts, :, :].rearrange("p u d -> p (u d)"),
                                 edge_attr[ds(it.index * GROUP, parts * U), :].rearrange("(p u) d -> p (u d)", u=U)
                                 ).then_inc(e_attr[j], 16)

                def group_added(it):
                    if it.per == 8:
                        g = Item(it.at, it.per // 2, (it.c - FIRST_FAST) // 2 + FASTER - 3, GROUPS)
                    else:
                        g = Item(it.at, it.per, it.c + lead, GROUPS)
                    j, n = g.of(2, r)
                    sp.wait_ge(e_added[j], 16 * U * (n + 1))
                    sp.sem_inc(sp_begun, 1)

                def load_accum(it):
                    j, n = it.of(2, r)
                    if r < 2:
                        sp.wait_ge(c_scaled[j], n)
                    else:
                        last = Item(it.at, 2 * it.per, 2 * it.c - 3, 2 * BLOCKS)
                        if it.at is not None or it.c >= 2:
                            q, m = last.of(2)
                            sp.wait_ge(m_turned[q], m + 1)
                    sp.dma_start(a_in[j][:, 0:S * widths[r]], rows(accums[r], it.index)
                                 ).then_inc(c_in[j], 16)

                def load_early(it):
                    group_added(it)
                    load_accum(it)

                def load_late(it):
                    all_done(sp, e_added, GROUPS, r + 1, 16 * U)
                    load_accum(it)

                def load_x(it):
                    j, n = it.of(4)
                    if r == 1:
                        q, m = Item(it.at, it.per, it.c - 4, BLOCKS).of(2)
                        if it.at is not None or it.c >= 4:
                            sp.wait_ge(d_shifted[q], m + 1)
                        parts = block_parts(it)
                        sp.dma_start(x_in[j][0:parts, :, :].rearrange("p s d -> p (s d)"),
                                     rows(x, it.index, parts)).then_inc(d_x[j], 16)
                    else:
                        if it.at is not None or it.c >= 4:
                            q, m = Item(it.at, 2 * it.per, 2 * it.c - 7, 2 * BLOCKS).of(2)
                            sp.wait_ge(m_out[q], m + 1)
                        sp.dma_start(x_in[j][:, :, :].rearrange("p s d -> p (s d)"),
                                     rows(skip, it.index)).then_inc(d_x[j], 16)

                def store(it):
                    q, m = it.of(4)
                    if r == 1:
                        sp.wait_ge(d_relu[q], m + 1)
                    else:
                        sp.wait_ge(c_applied[q], it.of(4, r + 1)[1] + 1)
                        sp.sem_inc(sp_begun, 1)
                        sp.wait_ge(c_column[q], m + 1)
                    for t in (tables[r + 1], accums[r + 1]):
                        sp.dma_start(rows(t, it.index), h_out[q][:, 0:S * widths[r + 1]]).then_inc(c_stored[q], 16)

                def store_skip(it):
                    j, n = it.of(2)
                    sp.wait_ge(d_skip[j], n + 1)
                    sp.dma_start(rows(skip, it.index), x_plus_h[j][:, :, :].rearrange("p s d -> p (s d)")
                                  ).then_inc(d_skip_stored[j], 16)

                def store_out(it):
                    k, o = Item(it.at, 2 * it.per, 2 * it.c + 1, 2 * BLOCKS).of(2)
                    j, n = it.of(4)
                    sp.wait_ge(m_out[k], o + 1)
                    parts = block_parts(it)
                    sp.dma_start(rows(out, it.index, parts), h_out[j][0:parts, 0:S * D]).then_inc(m_stored[j], 16)

                if r == 2:
                    all_done(sp, d_skip_stored, BLOCKS, 1, 16)
                stages = [groups(-3, load_row)]
                if r == 2:
                    stages.append(groups(-3, load_attr))
                over = at_step(-1, GROUPS + 3)
                stages += blocks(-1, load_early, 0, over) + blocks(-1, load_late, over)
                if r == 1:
                    stages += blocks(5, load_x)
                if r == 2:
                    stages += blocks(0, load_x)
                if r == 0:
                    stages += blocks(8, store)
                elif r == 1:
                    stages += blocks(11, store) + blocks(12, store_skip)
                else:
                    stages += blocks(4, store_out)
                run_steps(sp, 4, stages)
                if r == 2:
                    all_done(sp, m_stored, BLOCKS, 1, 16)
            rounds(sp, one_round)

        def shift_x(eng):
            def stage(it):
                j, n = it.of(2)
                q, m = it.of(4)
                eng.wait_ge(d_x[q], 16 * (m + 1))
                eng.wait_ge(d_summed[j], n)
                eng.tensor_tensor(shifted[j][:, :, :], x_in[q][:, :, :],
                                  shift1[:, :].unsqueeze(1).to_broadcast([P, S, D]), ALU.add
                                  ).then_inc(d_shifted[j], 1)
            return stage

        def add_skip(eng):
            def stage(it):
                j, n = it.of(2)
                q, m = it.of(4)
                eng.wait_ge(d_relu[q], m + 1)
                eng.wait_ge(d_skip_stored[j], 16 * n)
                eng.tensor_tensor(x_plus_h[j][:, :, :], x1[q][:, :, :], wide(h_out[q], D), ALU.add
                                  ).then_inc(d_skip[j], 1)
            return stage

        def evict(eng, copy, r):
            def stage(it):
                j, n = it.of(2, r)
                eng.wait_ge(c_turned[j], n + 1)
                eng.wait_ge(c_mm[j], n)
                w = widths[r]
                copy(turned[j][0:w, :].rearrange("p (h c) -> p h c", h=2), ps_turn[0:w, :, :]
                     ).then_inc(c_evicted[j], 1)
            return stage

        @block.gpsimd
        def _(pool):
            pool.memset(zeros[:, :], 0.0)
            pool.memset(neg_half[:, :], -0.5)
            pool.memset(ident[:, :], 0.0).then_inc(fill, 1)
            pool.iota(count_up[:, :], [[1, COLS]], base=0, channel_multiplier=0, allow_small_or_imprecise_dtypes=True)
            pool.iota(place[:, :], [[1, GROUP]], base=0, channel_multiplier=-U, allow_small_or_imprecise_dtypes=True)
            pool.iota(spare_f[:, :], [[P, U]], base=SPARE, channel_multiplier=1, allow_small_or_imprecise_dtypes=True)
            pool.iota(earliest[:, 0:FASTER - 3, :], [[BLOCK, FASTER - 3], [0, U]], base=-LEAD * BLOCK,
                      channel_multiplier=0, allow_small_or_imprecise_dtypes=True)
            pool.iota(earliest[:, FASTER - 3:GROUPS, :], [[2 * BLOCK, GROUPS - FASTER + 3], [0, U]],
                      base=FIRST_FAST * BLOCK, channel_multiplier=0, allow_small_or_imprecise_dtypes=True)
            pool.wait_ge(fill, 1)
            pool.affine_select(out=ident[:, :], in_=ident[:, :], compare_op=ALU.not_equal, fill=1.0,
                               base=0, pattern=[[-1, P]], channel_multiplier=1).then_inc(consts_ready, 1)

            def hot_parts(it):
                j, n = it.of(2)
                pool.wait_ge(hot_used[j], n)
                pool.wait_ge(part_taken[j], n + 1)
                pool.sem_inc(begun, 1)
                for u in range(HOT_V, U):
                    last = pool.tensor_scalar(hot_part[j][:, u, :], count_up[:, 0:P], part_slot[j][:, u:u + 1], None,
                                              ALU.is_equal)
                last.then_inc(hot_part_ready[j], 1)
            pool.wait_ge(consts_ready, 1)
            run_steps(pool, 4, [groups(0, hot_parts)])

            def power(var_ready, var_t, rstd_t, rstd_ready, passes=0):
                def stage(it):
                    j, n = it.of(4, passes)
                    pool.wait_ge(var_ready[j], n + 1)
                    pool.tensor_tensor(rstd_t[j][:, :], var_t[j][:, :], neg_half[:, :].to_broadcast([P, S]),
                                       ALU.pow).then_inc(rstd_ready[j], 1)
                return stage

            run_steps(pool, 8, [first_blocks(0, power(c_var, var, rstd, c_rstd))])
            pool.wait_ge(spare_zeroed, 32)
            all_done(pool, c_stored, BLOCKS, 1, 32)

            def one_round(r, lead):
                blocks, halves, at_step = behind(r, lead)
                if r > 0:
                    all_done(pool, c_stored, BLOCKS, r + 1, 32)

                def scatter(it):
                    j, n = it.of(2, r)
                    pool.wait_ge(e_summed[j], n + 1)
                    pool.wait_ge(e_rows[j], n + 1)
                    pool.wait_ge(e_added[1 - j], 16 * U * (n + j))
                    pool.sem_inc(begun, 1)
                    parts = edge_parts(it)
                    for u in range(U):
                        pool.indirect_dma_start(
                            out=accums[r][:, :],
                            out_offset=bass.IndirectOffsetOnAxis(ap=row_slot[j][0:parts, u:u + 1], axis=0),
                            in_=summed[j][0:parts, u, 0:widths[r]], in_offset=None, compute_op=ALU.add
                        ).then_inc(e_added[j], 16)

                def gather(it):
                    j, n = it.of(4, r)
                    pool.wait_ge(e_src[j], n + 1)
                    pool.sem_inc(begun, 1)
                    parts = edge_parts(it)
                    for u in range(U):
                        pool.indirect_dma_start(
                            out=got[j][0:parts, u, 0:widths[r]], out_offset=None, in_=tables[r][:, :],
                            in_offset=bass.IndirectOffsetOnAxis(ap=src_slot[j][0:parts, u:u + 1], axis=0)
                        ).then_inc(e_got[j], 16)
                stages = [groups(0, scatter), groups(-3, gather)]
                if r == 0:
                    stages += blocks(5, power(c_var, var, rstd, c_rstd, 1), at_step(5, FASTER))
                if r == 1:
                    late = at_step(0, GROUPS)
                    stages += blocks(5, power(c_var, var, rstd, c_rstd, 2), at_step(5, GROUPS))
                    stages += blocks(7, shift_x(pool)) + blocks(11, add_skip(pool), late)
                    stages += blocks(9, power(d_var, var_b, rstd_b, d_rstd), at_step(9, GROUPS))
                run_steps(pool, 4, stages)
            rounds(pool, one_round)

        @block.vector
        def _(dve):
            dve.memset(dst_i[:, PER_P - U:PER_P], PADDED)
            dve.memset(src_i[:, PER_P - U:PER_P], 0).then_inc(tail_clear, 1)
            dve.memset(left_dst[:, :], -1.0)
            for j in range(2):
                dve.memset(turned[j][D:D + 2, :], 1.0)
                dve.memset(hidden[j][D:D + 1, :], 1.0).then_inc(ones_ready, 1)
            dve.wait_ge(edges_in, 64)
            dve.tensor_copy(dst_f[:, :], dst_i[:, :])
            dve.tensor_scalar(part_i[:, :], dst_i[:, :], 3, P - 1, ALU.arith_shift_right, ALU.bitwise_and)
            dve.tensor_scalar(high_i[:, :], dst_i[:, :], 10, 3, ALU.arith_shift_right, ALU.logical_shift_left)
            dve.tensor_scalar(low_i[:, :], dst_i[:, :], S - 1, None, ALU.bitwise_and).then_inc(index_step, 1)
            dve.wait_ge(index_step, 1)
            by_group = dst_f[:, :].rearrange("p (g u) -> p g u", u=U)
            dve.tensor_scalar(last_dst[:, :], by_group[:, :, U - 1], 0.0, None, ALU.add).then_inc(last_ready, 1)
            dve.tensor_copy(part_f[:, :], part_i[:, :])
            dve.tensor_tensor(col_f[:, :], high_i[:, :], low_i[:, :], ALU.add).then_inc(index_step, 1)
            dve.wait_ge(consts_ready, 1)
            dve.tensor_tensor(slack[:, :], dst_f[:, :], earliest[:, :, :].rearrange("p g u -> p (g u)"),
                              ALU.subtract)
            dve.tensor_tensor(rise[:, :, 1:U], by_group[:, :, 1:U], by_group[:, :, 0:U - 1], ALU.subtract)
            dve.wait_ge(left_in, 16)
            dve.tensor_tensor(rise[:, :, 0], by_group[:, :, 0], left_dst[:, :], ALU.subtract).then_inc(least_ready, 1)
            dve.wait_ge(least_ready, 1)
            dve.tensor_tensor(slack[:, :], slack[:, :], rise[:, :, :].rearrange("p g u -> p (g u)"), ALU.min
                              ).then_inc(least_ready, 1)
            dve.wait_ge(least_ready, 2)
            dve.tensor_reduce(least[:, :], slack[:, :], op=ALU.min, axis=AX.X).then_inc(least_ready, 1)
            dve.tensor_tensor(dst_sp[:, :].rearrange("p (g u) -> p g u", u=U),
                              dst_f[:, :].rearrange("p (g u) -> p g u", u=U),
                              spare_f[:, :].unsqueeze(1).to_broadcast([P, GROUPS, U]), ALU.subtract)
            for u in range(U):
                dve.tensor_scalar(before[:, u, :], place[:, :], float(u), None, ALU.is_lt).then_inc(index_ready, 1)
            dve.wait_ge(index_ready, U)
            dve.scalar_tensor_tensor(out=first_sp[:, :], in0=rise[:, :, :].rearrange("p g u -> p (g u)"), scalar=0.0,
                                     in1=dst_sp[:, :], op0=ALU.not_equal, op1=ALU.mult).then_inc(index_ready, 1)
            dve.wait_ge(index_ready, U + 1)
            dve.tensor_tensor(row_i[:, :].rearrange("p (g u) -> p g u", u=U),
                              first_sp[:, :].rearrange("p (g u) -> p g u", u=U),
                              spare_f[:, :].unsqueeze(1).to_broadcast([P, GROUPS, U]), ALU.add
                              ).then_inc(index_ready, 1)
            dve.wait_ge(least_turned, 1)
            dve.tensor_reduce(least_all[:, :], ps_out[1][0:1, 1, 0:P], op=ALU.min, axis=AX.X).then_inc(least_ready, 1)
            dve.wait_ge(least_ready, 4)
            dve.tensor_scalar(ahead[:, :], least_all[:, :], 0.0, None, ALU.is_ge).then_inc(ahead_ready, 1)
            dve.wait_ge(index_step, 2)

            def one_hot(it):
                j, n = it.of(2)
                dve.wait_ge(hot_used[j], n)
                for u in range(U):
                    last = dve.tensor_scalar(hot_col[j][:, u, :], count_up[:, :], col_f[:, ds(it.index * U + u, 1)],
                                             None, ALU.is_equal)
                for u in range(HOT_V):
                    last = dve.tensor_scalar(hot_part[j][:, u, :], count_up[:, 0:P],
                                             part_f[:, ds(it.index * U + u, 1)], None, ALU.is_equal)
                last.then_inc(hot_ready[j], 1)
            run_steps(dve, 4, [groups(0, one_hot)])
            dve.wait_ge(weights_in, 16 * 12)
            dve.tensor_scalar(w1a[0:D, :], w1s[:, :], g0c[:, :], None, ALU.mult).then_inc(w1_ready, 1)
            dve.wait_ge(be0_w1, 1)
            dve.tensor_copy(w1a[D:D + 1, :], ps_out[1][0:1, 0, 0:D]).then_inc(w1_ready, 1)
            dve.tensor_scalar(deg[:, :].rearrange("p (h c) -> p h c", h=2), ps_turn[:, :, 0:HALF], 1.0, None,
                              ALU.add).then_inc(deg_ready, 1)
            dve.wait_ge(deg_root, 1)
            dve.reciprocal(dis[:, :], newton[:, :]).then_inc(newton_step, 1)
            dve.wait_ge(newton_step, 1)
            dve.tensor_tensor(newton[:, :], dis[:, :], dis[:, :], ALU.mult).then_inc(newton_step, 1)
            dve.wait_ge(newton_step, 2)
            dve.scalar_tensor_tensor(out=deg[:, :], in0=newton[:, :], scalar=-0.5, in1=deg[:, :],
                                     op0=ALU.mult, op1=ALU.mult).then_inc(newton_step, 1)
            dve.wait_ge(newton_step, 3)
            dve.scalar_tensor_tensor(out=dis[:, :], in0=deg[:, :], scalar=1.5, in1=dis[:, :],
                                     op0=ALU.add, op1=ALU.mult).then_inc(dis_ready, 1)

            def refine(root_t, about_t, root_ready, step, va, rstd_t, rstd_ready, passes):
                def operation(it, k):
                    j, _ = it.of(4)
                    about, var_j, to = about_t[j], va[j][:, :], rstd_t[j][:, :]
                    if k == 0:
                        dve.wait_ge(root_ready, it.index + 1)
                        dve.reciprocal(about[:, 0, :], root_t[j][:, :]).then_inc(step, 1)
                        return
                    dve.wait_ge(step, 3 * it.index + k)
                    if k == 1:
                        dve.tensor_tensor(about[:, 1, :], about[:, 0, :], about[:, 0, :], ALU.mult).then_inc(step, 1)
                    elif k == 2:
                        dve.scalar_tensor_tensor(out=about[:, 2, :], in0=about[:, 1, :], scalar=-0.5, in1=var_j,
                                                 op0=ALU.mult, op1=ALU.mult).then_inc(step, 1)
                    else:
                        dve.scalar_tensor_tensor(out=to, in0=about[:, 2, :], scalar=1.5, in1=about[:, 0, :],
                                                 op0=ALU.add, op1=ALU.mult).then_inc(rstd_ready[j], 1)
                return operation

            def variance(st, m2, md, ms, md2, va, step, src_t, var_ready, passes=0, between=None):
                def stage(it):
                    j, _ = it.of(4, passes)
                    s, done = step, 3 * (it.index + passes * BLOCKS)
                    rows_in = src_t[it.of(len(src_t))[0]]
                    for i in range(S):
                        last = dve.bn_stats(st[j][:, i, :], rows_in[:, i, :])
                        if between and i % 2 == 1:
                            between(Item(it.at, it.per, it.c - 1, it.total), i // 2)
                    last.then_inc(s, 1)
                    dve.wait_ge(s, done + 1)
                    dve.tensor_tensor(md[j][:, :], st[j][:, :, 1], st[j][:, :, 4], ALU.subtract).then_inc(s, 1)
                    dve.tensor_tensor(m2[j][:, :], st[j][:, :, 1], st[j][:, :, 4], ALU.add)
                    dve.scalar_tensor_tensor(out=ms[j][:, :], in0=st[j][:, :, 2], scalar=EPS * D,
                                             in1=st[j][:, :, 5], op0=ALU.add, op1=ALU.add)
                    dve.wait_ge(s, done + 2)
                    dve.scalar_tensor_tensor(out=md2[j][:, :], in0=md[j][:, :], scalar=0.25, in1=md[j][:, :],
                                             op0=ALU.mult, op1=ALU.mult).then_inc(s, 1)
                    dve.wait_ge(s, done + 3)
                    dve.scalar_tensor_tensor(out=va[j][:, :], in0=ms[j][:, :], scalar=1.0 / D, in1=md2[j][:, :],
                                             op0=ALU.mult, op1=ALU.add).then_inc(var_ready[j], 1)
                return stage

            var0 = variance(stats, mean2, mdiff, m2sum, mdiff2, var, c_step, x_ring, c_var)

            def stats0(it):
                k, n = it.of(8)
                dve.wait_ge(p0_x[k], 16 * (n + 1))
                var0(it)

            def scales0(it):
                j, n = it.of(4)
                dve.wait_ge(c_rstd[j], n + 1)
                dve.wait_ge(c_applied[j], n)
                dve.tensor_tensor(ln_a[j][:, :], rstd[j][:, :], dis[:, ds(it.index * S, S)], ALU.mult
                                  ).then_inc(c_ab[j], 1)
                dve.wait_ge(c_ab[j], 2 * n + 1)
                dve.scalar_tensor_tensor(out=ln_b[j][:, :], in0=mean2[j][:, :], scalar=-0.5, in1=ln_a[j][:, :],
                                         op0=ALU.mult, op1=ALU.mult).then_inc(c_ab[j], 1)

            def apply0(it):
                j, n = it.of(4)
                dve.wait_ge(c_ab[j], 2 * n + 2)
                for i in range(ROWS_V):
                    last = dve.tensor_scalar(tanhs[j][:, i, :], x_ring[it.of(8)[0]][:, i, :], ln_a[j][:, i:i + 1],
                                             ln_b[j][:, i:i + 1], ALU.mult, ALU.add)
                last.then_inc(c_tanh[j], 1)
            dve.wait_ge(dis_ready, 1)
            dve.wait_ge(index_ready, U + 2)
            run_steps(dve, 8, [first_blocks(2, scales0), first_blocks(0, stats0), first_blocks(2, apply0)])

            def copy_scaled(to, of):
                return dve.tensor_scalar(to, of, 1.0, None, ALU.mult)

            def one_round(r, lead):
                blocks, halves, at_step = behind(r, lead)

                def compare(it):
                    j, n = it.of(2, r)
                    dve.wait_ge(e_row[j], 16 * (n + 1))
                    dve.wait_ge(e_mm[j], n)
                    parts = edge_parts(it)
                    for u in range(U):
                        last = dve.tensor_scalar(same[j][0:parts, u, 0:parts * U], dst_row[j][0:parts, 0:parts * U],
                                                 dst_f[0:parts, ds(it.index * U + u, 1)], None, ALU.is_equal)
                    last.then_inc(e_same[j], 1)

                def choose(it):
                    j, n = it.of(2)
                    parts = edge_parts(it)
                    for u in range(U):
                        last = dve.scalar_tensor_tensor(
                            out=junk[0:parts, u, 0:parts * U], in0=dst_row[j][0:parts, 0:parts * U],
                            scalar=dst_f[0:parts, ds(it.index * U + u, 1)], in1=before[0:parts, u, 0:parts * U],
                            op0=ALU.is_equal, op1=ALU.mult, accum_out=earlier[j][0:parts, u:u + 1])
                    last.then_inc(e_step[j], 1)
                    dve.wait_ge(e_step[j], 3 * n + 1)
                    dve.scalar_tensor_tensor(out=chosen[j][:, :], in0=earlier[j][:, :], scalar=0.0,
                                             in1=dst_sp[:, ds(it.index * U, U)], op0=ALU.is_equal, op1=ALU.mult
                                             ).then_inc(e_step[j], 1)
                    dve.wait_ge(e_step[j], 3 * n + 2)
                    dve.tensor_tensor(row_i[:, ds(it.index * U, U)], chosen[j][:, :], spare_f[:, :], ALU.add
                                      ).then_inc(e_step[j], 1)

                def take_rows(it):
                    j, n = it.of(2, r)
                    if r == 0 and lead != LEAD:
                        dve.wait_ge(e_step[j], 3 * n + 3)
                    dve.wait_ge(e_added[j], 16 * U * n)
                    dve.tensor_scalar(row_slot[j][:, :], row_i[:, ds(it.index * U, U)], 0.0, None, ALU.add
                                      ).then_inc(e_rows[j], 1)

                def add_attr(it):
                    j, n = it.of(2)
                    q, m = it.of(4, r)
                    dve.wait_ge(e_got[q], 16 * U * (m + 1))
                    dve.wait_ge(e_attr[j], 16 * (n + 1))
                    dve.wait_ge(e_mm[j], n + 2 * len(range(j, GROUPS, 2)))
                    parts = edge_parts(it)
                    dve.tensor_tensor(message[j][0:parts, :, :], got[q][0:parts, :, 0:D], attr[j][0:parts, :, :],
                                      ALU.add).then_inc(e_sum[j], 1)
                    dve.wait_ge(e_sum[j], n + 1)
                    dve.tensor_scalar(message[j][0:parts, :, :], message[j][0:parts, :, :], 0.0, None, ALU.max
                                      ).then_inc(e_msg[j], 1)
                edge_stages = [groups(-2, compare)]
                if r == 0 and lead != LEAD:
                    edge_stages.append(groups(-2, choose))
                edge_stages.append(groups(-1, take_rows))
                if r == 2:
                    edge_stages.append(groups(-2, add_attr))
                stages = []

                def scale(it):
                    j, n = it.of(2, r)
                    dve.wait_ge(c_in[j], 16 * (n + 1))
                    dve.wait_ge(c_turned[j], n)
                    dve.tensor_tensor(wide(scaled[j], widths[r]), wide(a_in[j], widths[r]),
                                      dis[:, ds(it.index * S, S)].unsqueeze(2).to_broadcast([P, S, widths[r]]),
                                      ALU.mult).then_inc(c_scaled[j], 1)

                var1 = variance(stats, mean2, mdiff, m2sum, mdiff2, var, c_step, tanhs, c_var, r + 1)

                var1_refined = variance(stats, mean2, mdiff, m2sum, mdiff2, var, c_step, tanhs, c_var, r + 1,
                                        refine(root_a, about_a, root_a_ready, refine_a, var, rstd, c_rstd, r + 1))

                def stats1_refined(it):
                    j, n = it.of(4, r + 1)
                    dve.wait_ge(c_tanh[j], n + 1)
                    var1_refined(it)

                def stats1(it):
                    j, n = it.of(4, r + 1)
                    dve.wait_ge(c_tanh[j], n + 1)
                    var1(it)

                def root(it):
                    j, n = it.of(4, r + 1)
                    done = it.index * ROOT_OPS
                    dve.wait_ge(c_var[j], n + 1)
                    if it.at is not None or it.c > 0:
                        dve.wait_ge(root_step, done)
                    dve.tensor_scalar(guess[:, :], var[j][:, :].bitcast(i32), 1, None, ALU.logical_shift_right
                                      ).then_inc(root_step, 1)
                    dve.tensor_scalar(neg_var[:, :], var[j][:, :], -0.5, None, ALU.mult)
                    dve.wait_ge(root_step, done + 1)
                    dve.tensor_scalar(power_i[0][:, :], guess[:, :], -1.0, float(ROOT_GUESS), ALU.mult, ALU.add
                                      ).then_inc(root_step, 1)
                    for k in range(3):
                        y = power_i[k][:, :].bitcast(fp32)
                        to = rstd[j][:, :] if k == 2 else power_i[k + 1][:, :].bitcast(fp32)
                        dve.wait_ge(root_step, done + 3 * k + 2)
                        dve.tensor_tensor(square[:, :], y, y, ALU.mult).then_inc(root_step, 1)
                        dve.wait_ge(root_step, done + 3 * k + 3)
                        dve.tensor_tensor(gap[:, :], square[:, :], neg_var[:, :], ALU.mult).then_inc(root_step, 1)
                        dve.wait_ge(root_step, done + 3 * k + 4)
                        last = dve.scalar_tensor_tensor(out=to, in0=gap[:, :], scalar=1.5, in1=y,
                                                        op0=ALU.add, op1=ALU.mult)
                        last.then_inc(root_step if k < 2 else c_rstd[j], 1)

                def scales1(it):
                    j, n = it.of(4, r + 1)
                    dve.wait_ge(c_rstd[j], n + 1)
                    dve.wait_ge(c_applied[j], n)
                    if r == 1:
                        dve.tensor_scalar(ln_a[j][:, :], rstd[j][:, :], 1.0, None, ALU.mult).then_inc(c_ab[j], 1)
                    else:
                        dve.tensor_tensor(ln_a[j][:, :], rstd[j][:, :], dis[:, ds(it.index * S, S)], ALU.mult
                                          ).then_inc(c_ab[j], 1)
                    dve.wait_ge(c_ab[j], 2 * n + 1)
                    dve.scalar_tensor_tensor(out=ln_b[j][:, :], in0=mean2[j][:, :], scalar=-0.5, in1=ln_a[j][:, :],
                                             op0=ALU.mult, op1=ALU.mult).then_inc(c_ab[j], 1)

                def column(it):
                    j, n = it.of(4)
                    _, m = it.of(4, r + 1)
                    dve.wait_ge(c_stored[j], 32 * m)
                    dve.tensor_scalar(wide(h_out[j], WIDE)[:, :, D], dis[:, ds(it.index * S, S)], 1.0, None,
                                      ALU.mult).then_inc(c_column[j], 1)

                def gain(it):
                    j, n = it.of(2)
                    q, m = it.of(4, r + 1)
                    dve.wait_ge(c_applied[q], m + 1)
                    dve.wait_ge(d_summed[j], n)
                    dve.tensor_tensor(gained[j][:, :, :], normed[j][:, :, :],
                                      gain1[:, :].unsqueeze(1).to_broadcast([P, S, D]), ALU.mult
                                      ).then_inc(d_gained[j], 1)

                var2 = variance(stats_b, mean2_b, mdiff_b, m2sum_b, mdiff2_b, var_b, d_step, x1, d_var)
                var2_refined = variance(stats_b, mean2_b, mdiff_b, m2sum_b, mdiff2_b, var_b, d_step, x1, d_var, 0,
                                        refine(root_b, about_b, root_b_ready, refine_b, var_b, rstd_b, d_rstd, 0))

                def add_residual(it):
                    j, n = it.of(2)
                    q, m = it.of(4)
                    dve.wait_ge(d_gained[j], n + 1)
                    dve.wait_ge(d_shifted[j], n + 1)
                    k, o = Item(it.at, it.per, it.c - 4, BLOCKS).of(2)
                    if it.at is not None or it.c >= 4:
                        dve.wait_ge(d_skip[k], o + 1)
                    dve.tensor_tensor(x1[q][:, :, :], gained[j][:, :, :], shifted[j][:, :, :], ALU.add
                                      ).then_inc(d_summed[j], 1)
                    dve.wait_ge(d_summed[j], n + 1)

                def residual(it):
                    add_residual(it)
                    var2(it)

                def residual_refined(it):
                    add_residual(it)
                    var2_refined(it)

                def scales2(it):
                    j, n = it.of(4)
                    dve.wait_ge(d_rstd[j], n + 1)
                    dve.wait_ge(d_relu[j], n)
                    dve.scalar_tensor_tensor(out=ln_b_b[j][:, :], in0=mean2_b[j][:, :], scalar=-0.5,
                                             in1=rstd_b[j][:, :], op0=ALU.mult, op1=ALU.mult).then_inc(d_ab, 1)

                def finish(it):
                    h, n = it.of(2)
                    b = Item(it.at, it.per // 2, it.c // 2, BLOCKS)
                    j, m = b.of(4)
                    dve.wait_ge(m_mm2[h], n + 1)
                    if h == 0:
                        dve.wait_ge(d_x[j], 16 * (b.of(4, 1)[1] + 1))
                        dve.wait_ge(m_stored[j], 16 * m)
                    dve.scalar_tensor_tensor(
                        out=h_out[j][:, h * HS:(h + 1) * HS], in0=ps_out[1][:, h, 0:HS], scalar=0.0,
                        in1=x_in[j][:, :, :].rearrange("p s d -> p (s d)")[:, h * HS:(h + 1) * HS],
                        op0=ALU.max, op1=ALU.add).then_inc(m_out[h], 1)

                if r == 0:
                    stages += blocks(0, scale) + blocks(6, scales1)
                    stages += blocks(5, root, 0, at_step(5, FASTER))
                    stages += blocks(6, column) + blocks(4, stats1)
                    stages += blocks(1, evict(dve, copy_scaled, r), at_step(1, GROUPS))
                elif r == 1:
                    early = at_step(0, GROUPS)
                    stages += blocks(0, scale) + blocks(6, scales1) + blocks(8, gain)
                    stages += blocks(10, scales2) + blocks(11, add_skip(dve), 0, early)
                    root_to_a, root_to_b = at_step(5, GROUPS), at_step(9, GROUPS)
                    stages += blocks(4, stats1, 0, 1) + blocks(4, stats1_refined, 1, root_to_a + 1)
                    stages += blocks(4, stats1, max(1, root_to_a + 1))
                    stages += blocks(8, residual, 0, 1) + blocks(8, residual_refined, 1, root_to_b + 1)
                    stages += blocks(8, residual, max(1, root_to_b + 1))
                else:
                    stages += halves(5, finish)
                run_steps(dve, 4, stages + edge_stages)
            rounds(dve, one_round)

        @block.scalar
        def _(act):
            act.wait_ge(index_step, 2)

            def take_parts(it):
                j, n = it.of(2)
                act.wait_ge(hot_part_ready[j], n)
                act.copy(part_slot[j][:, :], part_f[:, ds(it.index * U, U)]).then_inc(part_taken[j], 1)
            run_steps(act, 4, [groups(0, take_parts)])
            act.wait_ge(deg_ready, 1)
            act.activation(newton[:, :], deg[:, :], ACT.Sqrt).then_inc(deg_root, 1)

            def relu0(it):
                j, n = it.of(4)
                act.wait_ge(c_tanh[j], n + 1)
                act.wait_ge(c_ab[j], 2 * n + 2)
                act.wait_ge(c_stored[j], 32 * n)
                for i in range(ROWS_V, S):
                    act.activation(wide(h_out[j], D)[:, i, :], x_ring[it.of(8)[0]][:, i, :], ACT.Relu,
                                   bias=ln_b[j][:, i:i + 1], scale=ln_a[j][:, i:i + 1])
                act.activation(h_out[j][:, 0:ROWS_V * D], tanhs[j][:, 0:ROWS_V, :].rearrange("p s d -> p (s d)"), ACT.Relu
                               ).then_inc(c_applied[j], 1)

            run_steps(act, 8, [first_blocks(2, relu0)])

            def root_of(var_ready, va, root_t, root_ready, passes):
                def stage(it):
                    j, n = it.of(4, passes)
                    act.wait_ge(var_ready[j], n + 1)
                    act.activation(root_t[j][:, :], va[j][:, :], ACT.Sqrt).then_inc(root_ready, 1)
                return stage

            def one_round(r, lead):
                blocks, halves, at_step = behind(r, lead)

                def take_src(it):
                    j, n = it.of(4, r)
                    act.wait_ge(e_got[j], 16 * U * n)
                    if it.at is not None or it.c >= 4:
                        q, m = Item(it.at, it.per, it.c - 4, GROUPS).of(2, r)
                        act.wait_ge(e_mm[q], m + 1)
                    act.copy(src_slot[j][:, :], src_i[:, ds(it.index * U, U)]).then_inc(e_src[j], 1)

                def evict_sums(it):
                    j, n = it.of(2, r)
                    act.wait_ge(e_mm[j], n + 1)
                    act.wait_ge(e_added[j], 16 * U * n)
                    parts = edge_parts(it)
                    act.copy(summed[j][0:parts, :, 0:widths[r]],
                             ps_sum[0:parts, j, 0:U * widths[r]].rearrange("p (u d) -> p u d", u=U)
                             ).then_inc(e_summed[j], 1)
                edge_stages = [groups(-1, evict_sums), groups(-4, take_src)]
                stages = []

                def tanh(it):
                    j, n = it.of(2, r)
                    q, m = it.of(4, r + 1)
                    act.wait_ge(c_mm[j], n + 1)
                    act.wait_ge(c_applied[q], m)
                    act.activation(tanhs[q][:, :, :].rearrange("p (h s) d -> p h (s d)", h=2),
                                   ps_out[j][:, :, 0:HS], ACT.Tanh).then_inc(c_tanh[q], 1)

                def apply(it):
                    q, m = it.of(4, r + 1)
                    act.wait_ge(c_ab[q], 2 * m + 2)
                    if r == 1:
                        j, n = it.of(2)
                        act.wait_ge(d_gained[j], n)
                        to = normed[j][:, :, :]
                    else:
                        act.wait_ge(c_stored[q], 32 * m)
                        to = wide(h_out[q], WIDE)
                    for i in range(S):
                        last = act.activation(to[:, i, 0:D], tanhs[q][:, i, :], ACT.Identity,
                                              bias=ln_b[q][:, i:i + 1], scale=ln_a[q][:, i:i + 1])
                    last.then_inc(c_applied[q], 1)

                def apply2(it):
                    q, m = it.of(4)
                    _, m_both = it.of(4, r + 1)
                    act.wait_ge(d_ab, it.index + 1)
                    act.wait_ge(c_stored[q], 32 * m_both)
                    if it.at is not None or it.c >= 4:
                        k, o = Item(it.at, it.per, it.c - 4, BLOCKS).of(2)
                        act.wait_ge(d_skip[k], o + 1)
                    for i in range(S):
                        last = act.activation(wide(h_out[q], D)[:, i, :], x1[q][:, i, :], ACT.Relu,
                                              bias=ln_b_b[q][:, i:i + 1], scale=rstd_b[q][:, i:i + 1])
                    last.then_inc(d_relu[q], 1)

                def evict_last(it):
                    j, h, n = half(it)
                    act.wait_ge(m_turned[h], n + 1)
                    if four_back(it):
                        act.wait_ge(m_mm1[h], n - 1)
                    act.copy(turned[j][0:D, h * HB:(h + 1) * HB], ps_turn[0:D, h, :]).then_inc(m_evicted[h], 1)

                def hide(it):
                    j, h, n = half(it)
                    act.wait_ge(m_mm1[h], n + 1)
                    if four_back(it):
                        act.wait_ge(m_mm2[h], n - 1)
                    act.activation(hidden[j][0:D, h * HB:(h + 1) * HB], ps_out[0][0:D, h, :],
                                   ACT.Relu, bias=mb1s[:, :]).then_inc(m_hidden[h], 1)

                if r == 0:
                    stages += blocks(1, evict(act, act.copy, r), 0, at_step(1, GROUPS))
                    stages += blocks(7, apply) + blocks(3, tanh)
                elif r == 1:
                    stages += blocks(5, root_of(c_var, var, root_a, root_a_ready, 2), 0, at_step(5, GROUPS))
                    stages += blocks(9, root_of(d_var, var_b, root_b, root_b_ready, 0), 0, at_step(9, GROUPS))
                    stages += blocks(1, evict(act, act.copy, r)) + blocks(7, apply) + blocks(3, tanh)
                    stages += blocks(10, apply2)
                else:
                    stages += halves(1, evict_last) + halves(3, hide)
                run_steps(act, 4, stages + edge_stages)
            rounds(act, one_round)

        @block.tensor
        def _(pe):
            pe.wait_ge(least_ready, 3)
            pe.wait_ge(consts_ready, 1)
            pe.transpose(ps_out[1][0:1, 1, 0:P], least[:, :], ident[:, :]).then_inc(least_turned, 1)

            def count(it):
                j, n = it.of(2)
                pe.wait_ge(hot_ready[j], n + 1)
                pe.wait_ge(hot_part_ready[j], n + 1)
                first = it.at is None and it.c == 0
                parts = edge_parts(it)
                for u in range(U):
                    for h in range(2):
                        last = pe.matmul(ps_turn[:, h, 0:HALF], hot_part[j][0:parts, u, :],
                                         hot_col[j][0:parts, u, h * HALF:(h + 1) * HALF],
                                         start=first and u == 0, stop=it.last() and u == U - 1)
                last.then_inc(hot_used[j], 1)
            run_steps(pe, 4, [groups(0, count)])
            pe.wait_ge(weights_in, 16 * 12)
            pe.matmul(ps_out[1][0:1, 0, 0:D], be0c[:, :], w1s[:, :], start=True, stop=True).then_inc(be0_w1, 1)
            pe.wait_ge(w1_ready, 2)
            pe.wait_ge(ones_ready, 2)

            def one_round(r, lead):
                blocks, halves, at_step = behind(r, lead)

                def sums(it):
                    j, n = it.of(2, r)
                    q, m = it.of(4, r)
                    pe.wait_ge(e_same[j], n + 1)
                    if r == 2:
                        pe.wait_ge(e_msg[j], it.of(2)[1] + 1)
                        rhs = message[j]
                    else:
                        pe.wait_ge(e_got[q], 16 * U * (m + 1))
                        rhs = got[q]
                    pe.wait_ge(e_summed[j], n)
                    parts, w = edge_parts(it), widths[r]
                    for i in range(U):
                        for u in range(U):
                            last = pe.matmul(
                                ps_sum[0:parts, j, i * w:(i + 1) * w],
                                same[j][0:parts, u, 0:parts * U].rearrange("p (q i) -> p i q", i=U)[:, i, :],
                                rhs[0:parts, u, 0:w], start=u == 0, stop=u == U - 1)
                    last.then_inc(e_mm[j], 1)

                def turn(it):
                    j, n = it.of(2, r)
                    w = widths[r]
                    pe.wait_ge(c_scaled[j], n + 1)
                    pe.wait_ge(c_evicted[1 - j], n + j)
                    for i in range(S):
                        last = pe.transpose(ps_turn[0:w, i // 4, (i % 4) * P:(i % 4 + 1) * P],
                                            wide(scaled[j], w)[:, i, :], ident[:, :])
                    last.then_inc(c_turned[j], 1)

                def project(it):
                    j, n = it.of(2, r)
                    w = widths[r]
                    pe.wait_ge(c_evicted[j], n + 1)
                    k, o = Item(it.at, it.per, it.c - 2, BLOCKS).of(4, r + 1)
                    if it.at is not None or it.c >= 2:
                        pe.wait_ge(c_tanh[k], o + 1)
                    for i in range(S):
                        last = pe.matmul(ps_out[j][:, i // 4, (i % 4) * D:(i % 4 + 1) * D],
                                         turned[j][0:w + 1, i * P:(i + 1) * P], (w0a, w1a)[r][:, :],
                                         start=True, stop=True)
                    last.then_inc(c_mm[j], 1)

                def turn_last(it):
                    j, h, n = half(it)
                    _, m = Item(it.at, it.per // 2, it.c // 2, BLOCKS).of(2, r)
                    pe.wait_ge(c_in[j], 16 * (m + 1))
                    pe.wait_ge(m_evicted[h], n)
                    for i in range(S // 2):
                        last = pe.transpose(ps_turn[0:D, h, i * P:(i + 1) * P],
                                            wide(a_in[j], D)[:, h * S // 2 + i, :], ident[:, :])
                    last.then_inc(m_turned[h], 1)

                def hide_mm(it):
                    j, h, n = half(it)
                    pe.wait_ge(m_evicted[h], n + 1)
                    pe.wait_ge(m_hidden[h], n)
                    pe.matmul(ps_out[0][0:D, h, :], mw1s[:, :], turned[j][0:D, h * HB:(h + 1) * HB],
                              start=True, stop=True).then_inc(m_mm1[h], 1)

                def project_last(it):
                    j, h, n = half(it)
                    pe.wait_ge(m_hidden[h], n + 1)
                    pe.wait_ge(m_out[h], n)
                    for i in range(S // 2):
                        c = h * HB + i * P
                        last = pe.matmul(ps_out[1][:, h, i * D:(i + 1) * D], hidden[j][:, c:c + P], mw2a[:, :],
                                         start=True, stop=True)
                    last.then_inc(m_mm2[h], 1)

                stages = []
                if r < 2:
                    stages += blocks(1, turn) + blocks(2, project)
                else:
                    stages += halves(0, turn_last) + halves(2, hide_mm) + halves(4, project_last)
                run_steps(pe, 4, stages + [groups(-1, sums)])
            rounds(pe, one_round)


_INS = ['x', 'src', 'dst', 'edge_attr_96', 'L0_gnn_W0', 'L0_gnn_b0', 'L0_gnn_g0', 'L0_gnn_be0', 'L0_gnn_W1',
        'L0_gnn_b1', 'L0_gnn_g1', 'L0_gnn_be1', 'L1_gnn_W1', 'L1_gnn_b1', 'L1_gnn_W2', 'L1_gnn_b2']


def kernel(**inputs):
    import numpy as np
    import concourse.bacc as bacc
    from concourse.bass_utils import run_bass_kernel_spmd

    nc = bacc.Bacc("TRN2", target_bir_lowering=False, num_devices=1)
    arrays, args = {}, []
    for name in _INS:
        a = np.ascontiguousarray(inputs[name])
        arrays[f"in_{name}"] = a
        args.append(nc.dram_tensor(f"in_{name}", a.shape, mybir.dt.from_np(a.dtype), kind="ExternalInput").ap())
    x = inputs["x"]
    args.append(nc.dram_tensor("out_0", x.shape, mybir.dt.float32, kind="ExternalOutput").ap())
    gnn_kernel(nc, *args)
    return run_bass_kernel_spmd(nc, [arrays], core_ids=[0]).results[0]["out_0"]
```
